# Optimizing a Trainium2 kernel written in Bass

```python
import numpy as np
import jax
import jax.numpy as jnp

def _softmax(x, axis=-1):
    return jax.nn.softmax(x, axis=axis)

def _gelu(x):
    return jax.nn.gelu(x, approximate=True)

def _silu(x):
    return jax.nn.silu(x)

def _sigmoid(x):
    return jax.nn.sigmoid(x)

def _layernorm(x, axis=-1, eps=1e-05):
    m = jnp.mean(x, axis=axis, keepdims=True)
    v = jnp.var(x, axis=axis, keepdims=True)
    return (x - m) / jnp.sqrt(v + eps)

def _scatter_add(tgt, idx, src, axis=0):
    return tgt.at[idx].add(src)

def _segment_sum(src, seg, n):
    return jax.ops.segment_sum(src, seg, n)
kernel_name = 'mk_audio_tower_d2_tok_aud1d256_r4_f9e6d2'

def setup_inputs(seed: int=0):
    np.random.seed(seed)
    _w = jnp.asarray

    def _rec_inputs():
        import jax
        import jax.numpy as jnp
        _rk = jax.random.key(seed)
        x = -0.000292821 + 1.00034 * jax.random.normal(jax.random.fold_in(_rk, 1), (64, 8192), jnp.float32)
        return x
    x = _rec_inputs()

    def _L0_tok_setup():
        import jax, jax.numpy as jnp
        import numpy as np
        EPS = 1e-05

        def _conv1d(x, W, b, stride, pad):
            y = jax.lax.conv_general_dilated(x, W, (stride,), [(pad, pad)], dimension_numbers=('NCH', 'OIH', 'NCH'))
            return y + b[None, :, None]

        def _bn(x, g, b, m, v):
            return (x - m[None, :, None]) * (g * jax.lax.rsqrt(v + EPS))[None, :, None] + b[None, :, None]

        def _maxpool(x, k):
            B, C, L = x.shape
            return x.reshape(B, C, L // k, k).max(axis=-1)

        def _self_attn(x, Wq, bq, Wk, bk, Wv, bv, gamma):
            q = jnp.einsum('oc,bcl->bol', Wq, x) + bq[None, :, None]
            k = jnp.einsum('oc,bcl->bol', Wk, x) + bk[None, :, None]
            v = jnp.einsum('oc,bcl->bol', Wv, x) + bv[None, :, None]
            energy = jnp.einsum('bci,bcj->bij', q, k)
            attn = jax.nn.softmax(energy, axis=-1)
            out = jnp.einsum('bcj,bij->bci', v, attn)
            return gamma * out + x
        key = jax.random.key(seed)
        ks = jax.random.split(key, 32)
        B, D = (128, 8192)
        r = lambda i, shape, s=0.1: jax.random.normal(ks[i], shape, jnp.float32) * s
        return {'x': jax.random.normal(ks[0], (B, D), jnp.float32), 'w1': r(1, (16, 2, 3)), 'b1': r(2, (16,)), 'g1': 1.0 + r(3, (16,)), 'be1': r(4, (16,)), 'm1': r(5, (16,)), 'v1': 0.5 + jax.random.uniform(ks[6], (16,), jnp.float32), 'w2': r(7, (64, 16, 3)), 'b2': r(8, (64,)), 'g2': 1.0 + r(9, (64,)), 'be2': r(10, (64,)), 'm2': r(11, (64,)), 'v2': 0.5 + jax.random.uniform(ks[12], (64,), jnp.float32), 'wq': r(13, (8, 64)), 'bq': r(14, (8,)), 'wk': r(15, (8, 64)), 'bk': r(16, (8,)), 'wv': r(17, (64, 64)), 'bv': r(18, (64,)), 'gamma': jnp.float32(0.7), 'w3': r(19, (128, 64, 4)), 'b3': r(20, (128,)), 'g3': 1.0 + r(21, (128,)), 'be3': r(22, (128,)), 'm3': r(23, (128,)), 'v3': 0.5 + jax.random.uniform(ks[24], (128,), jnp.float32)}
    _L0_tok_all = _L0_tok_setup()
    _L0_tok_in = {k: v for k, v in _L0_tok_all.items() if k in ('w1', 'b1', 'g1', 'be1', 'm1', 'v1', 'w2', 'b2', 'g2', 'be2', 'm2', 'v2', 'wq', 'bq', 'wk', 'bk', 'wv', 'bv', 'gamma', 'w3', 'b3', 'g3', 'be3', 'm3', 'v3')}
    del _L0_tok_all

    def _L0_attn_setup():
        import jax, jax.numpy as jnp
        import numpy as np
        HEADS = 8
        EPS = 1e-05

        def _ln(t, w, b, headc):
            m = jnp.mean(t, axis=-1, keepdims=True)
            d = t - m
            std = jnp.sqrt(jnp.sum(d * d, axis=-1, keepdims=True) / (headc - 1))
            return w * (d / (std + EPS)) + b
        key = jax.random.key(seed)
        B, N, C = (32, 1024, 64)
        headc = C // HEADS
        x = jax.random.normal(key, (B, N, C), dtype=jnp.float32)
        return {'x': x, 'kln_weight': jnp.ones((HEADS, 1, headc), dtype=jnp.float32), 'kln_bias': jnp.zeros((HEADS, 1, headc), dtype=jnp.float32), 'vln_weight': jnp.ones((HEADS, 1, headc), dtype=jnp.float32), 'vln_bias': jnp.zeros((HEADS, 1, headc), dtype=jnp.float32)}
    _L0_attn_all = _L0_attn_setup()
    _L0_attn_in = {k: v for k, v in _L0_attn_all.items() if k in ('kln_weight', 'kln_bias', 'vln_weight', 'vln_bias')}
    del _L0_attn_all

    def _L0_ffn_setup():
        import jax, jax.numpy as jnp
        import numpy as np
        B, T, C = (64, 96, 64)
        NH, NKV = (4, 2)
        HD = C // NH
        NREP = NH // NKV
        NE, TOPK = (8, 2)
        HID = int(8 / 3 * C)
        EPS_RMS = 1e-06

        def _rope_tables(t_len):
            inv_freq = 1.0 / 10000.0 ** (np.arange(0, HD, 2, dtype=np.float32) / HD)
            t = np.arange(t_len, dtype=np.float32)
            freqs = np.outer(t, inv_freq)
            emb = np.concatenate([freqs, freqs], axis=-1)
            return (jnp.asarray(np.cos(emb)), jnp.asarray(np.sin(emb)))

        def _rotate_half(x):
            h = x.shape[-1] // 2
            return jnp.concatenate([-x[..., h:], x[..., :h]], axis=-1)

        def _rmsnorm(v, w):
            return v * jax.lax.rsqrt(jnp.mean(v * v, axis=-1, keepdims=True) + EPS_RMS) * w
        key = jax.random.key(seed)
        ks = jax.random.split(key, 10)
        s = lambda k, shape: jax.random.normal(k, shape, jnp.float32) * 0.02
        return {'x': jax.random.normal(ks[0], (B, T, C), jnp.float32), 'ln1_w': jnp.ones((C,), jnp.float32), 'ln2_w': jnp.ones((C,), jnp.float32), 'wq': s(ks[1], (NH * HD, C)), 'wk': s(ks[2], (NKV * HD, C)), 'wv': s(ks[3], (NKV * HD, C)), 'wo': s(ks[4], (C, C)), 'router_w': s(ks[5], (NE, C)), 'w1': s(ks[6], (NE, HID, C)), 'w2': s(ks[7], (NE, C, HID)), 'w3': s(ks[8], (NE, HID, C))}
    _L0_ffn_all = _L0_ffn_setup()
    _L0_ffn_in = {k: v for k, v in _L0_ffn_all.items() if k in ('ln1_w', 'ln2_w', 'wq', 'wk', 'wv', 'wo', 'router_w', 'w1', 'w2', 'w3')}
    del _L0_ffn_all

    def _L1_attn_setup():
        import jax, jax.numpy as jnp
        import numpy as np
        B, L, D = (4, 1024, 64)
        key = jax.random.key(seed)
        kx, kq, kk, kv, ko = jax.random.split(key, 5)
        std = 0.02
        return {'x': jax.random.normal(kx, (B, L, D), dtype=jnp.float32), 'Wq': std * jax.random.normal(kq, (D, D), dtype=jnp.float32), 'Wk': std * jax.random.normal(kk, (D, D), dtype=jnp.float32), 'Wv': std * jax.random.normal(kv, (D, D), dtype=jnp.float32), 'Wo': std * jax.random.normal(ko, (D, D), dtype=jnp.float32)}
    _L1_attn_all = _L1_attn_setup()
    _L1_attn_in = {k: v for k, v in _L1_attn_all.items() if k in ('Wq', 'Wk', 'Wv', 'Wo')}
    del _L1_attn_all

    def _L1_ffn_setup():
        import jax, jax.numpy as jnp
        import numpy as np
        NUM_EXPERTS = 8
        TOP_K = 2
        B, S, D = (8, 2048, 64)

        def _moe(tokens, router_w, w1, b1, w2, b2):
            N = tokens.shape[0]
            E = router_w.shape[0]
            logits = tokens.astype(jnp.float32) @ router_w.astype(jnp.float32).T
            probs = jax.nn.softmax(logits, axis=-1)
            rw, re = jax.lax.top_k(probs, TOP_K)
            if TOP_K > 1:
                rw = rw / jnp.maximum(rw.sum(-1, keepdims=True), 1e-12)
            rw = rw.astype(tokens.dtype)
            combine = jnp.zeros((N, E), tokens.dtype).at[jnp.arange(N)[:, None], re].set(rw)
            out = tokens
            for e in range(E):
                h = jax.nn.gelu(tokens @ w1[e] + b1[e], approximate=False)
                y = h @ w2[e] + b2[e]
                out = out + combine[:, e:e + 1] * y
            return out
        key = jax.random.key(seed)
        ks = jax.random.split(key, 4)
        scale = 1.0 / np.sqrt(D).astype(np.float32)
        return {'input_embeddings': jax.random.normal(ks[0], (B, S, D), jnp.float32), 'router_w': jax.random.normal(ks[1], (NUM_EXPERTS, D), jnp.float32) * scale, 'w1': jax.random.normal(ks[2], (NUM_EXPERTS, D, D), jnp.float32) * scale, 'b1': jnp.zeros((NUM_EXPERTS, D), jnp.float32), 'w2': jax.random.normal(ks[3], (NUM_EXPERTS, D, D), jnp.float32) * scale, 'b2': jnp.zeros((NUM_EXPERTS, D), jnp.float32)}
    _L1_ffn_all = _L1_ffn_setup()
    _L1_ffn_in = {k: v for k, v in _L1_ffn_all.items() if k in ('router_w', 'w1', 'b1', 'w2', 'b2')}
    del _L1_ffn_all
    return {'x': x, 'L0_tok_w1': _L0_tok_in['w1'], 'L0_tok_b1': _L0_tok_in['b1'], 'L0_tok_g1': _L0_tok_in['g1'], 'L0_tok_be1': _L0_tok_in['be1'], 'L0_tok_m1': _L0_tok_in['m1'], 'L0_tok_v1': _L0_tok_in['v1'], 'L0_tok_w2': _L0_tok_in['w2'], 'L0_tok_b2': _L0_tok_in['b2'], 'L0_tok_g2': _L0_tok_in['g2'], 'L0_tok_be2': _L0_tok_in['be2'], 'L0_tok_m2': _L0_tok_in['m2'], 'L0_tok_v2': _L0_tok_in['v2'], 'L0_tok_wq': _L0_tok_in['wq'], 'L0_tok_bq': _L0_tok_in['bq'], 'L0_tok_wk': _L0_tok_in['wk'], 'L0_tok_bk': _L0_tok_in['bk'], 'L0_tok_wv': _L0_tok_in['wv'], 'L0_tok_bv': _L0_tok_in['bv'], 'L0_tok_gamma': _L0_tok_in['gamma'], 'L0_tok_w3': _L0_tok_in['w3'], 'L0_tok_b3': _L0_tok_in['b3'], 'L0_tok_g3': _L0_tok_in['g3'], 'L0_tok_be3': _L0_tok_in['be3'], 'L0_tok_m3': _L0_tok_in['m3'], 'L0_tok_v3': _L0_tok_in['v3'], 'L0_attn_kln_weight': _L0_attn_in['kln_weight'], 'L0_attn_kln_bias': _L0_attn_in['kln_bias'], 'L0_attn_vln_weight': _L0_attn_in['vln_weight'], 'L0_attn_vln_bias': _L0_attn_in['vln_bias'], 'L0_ffn_ln1_w': _L0_ffn_in['ln1_w'], 'L0_ffn_ln2_w': _L0_ffn_in['ln2_w'], 'L0_ffn_wq': _L0_ffn_in['wq'], 'L0_ffn_wk': _L0_ffn_in['wk'], 'L0_ffn_wv': _L0_ffn_in['wv'], 'L0_ffn_wo': _L0_ffn_in['wo'], 'L0_ffn_router_w': _L0_ffn_in['router_w'], 'L0_ffn_w1': _L0_ffn_in['w1'], 'L0_ffn_w2': _L0_ffn_in['w2'], 'L0_ffn_w3': _L0_ffn_in['w3'], 'L1_attn_Wq': _L1_attn_in['Wq'], 'L1_attn_Wk': _L1_attn_in['Wk'], 'L1_attn_Wv': _L1_attn_in['Wv'], 'L1_attn_Wo': _L1_attn_in['Wo'], 'L1_ffn_router_w': _L1_ffn_in['router_w'], 'L1_ffn_w1': _L1_ffn_in['w1'], 'L1_ffn_b1': _L1_ffn_in['b1'], 'L1_ffn_w2': _L1_ffn_in['w2'], 'L1_ffn_b2': _L1_ffn_in['b2']}

def reference(x, L0_tok_w1, L0_tok_b1, L0_tok_g1, L0_tok_be1, L0_tok_m1, L0_tok_v1, L0_tok_w2, L0_tok_b2, L0_tok_g2, L0_tok_be2, L0_tok_m2, L0_tok_v2, L0_tok_wq, L0_tok_bq, L0_tok_wk, L0_tok_bk, L0_tok_wv, L0_tok_bv, L0_tok_gamma, L0_tok_w3, L0_tok_b3, L0_tok_g3, L0_tok_be3, L0_tok_m3, L0_tok_v3, L0_attn_kln_weight, L0_attn_kln_bias, L0_attn_vln_weight, L0_attn_vln_bias, L0_ffn_ln1_w, L0_ffn_ln2_w, L0_ffn_wq, L0_ffn_wk, L0_ffn_wv, L0_ffn_wo, L0_ffn_router_w, L0_ffn_w1, L0_ffn_w2, L0_ffn_w3, L1_attn_Wq, L1_attn_Wk, L1_attn_Wv, L1_attn_Wo, L1_ffn_router_w, L1_ffn_w1, L1_ffn_b1, L1_ffn_w2, L1_ffn_b2):
    import jax
    import jax.numpy as jnp

    def _L0_tok_ref(x, w1, b1, g1, be1, m1, v1, w2, b2, g2, be2, m2, v2, wq, bq, wk, bk, wv, bv, gamma, w3, b3, g3, be3, m3, v3):
        import jax, jax.numpy as jnp
        import numpy as np
        EPS = 1e-05

        def _conv1d(x, W, b, stride, pad):
            y = jax.lax.conv_general_dilated(x, W, (stride,), [(pad, pad)], dimension_numbers=('NCH', 'OIH', 'NCH'))
            return y + b[None, :, None]

        def _bn(x, g, b, m, v):
            return (x - m[None, :, None]) * (g * jax.lax.rsqrt(v + EPS))[None, :, None] + b[None, :, None]

        def _maxpool(x, k):
            B, C, L = x.shape
            return x.reshape(B, C, L // k, k).max(axis=-1)

        def _self_attn(x, Wq, bq, Wk, bk, Wv, bv, gamma):
            q = jnp.einsum('oc,bcl->bol', Wq, x) + bq[None, :, None]
            k = jnp.einsum('oc,bcl->bol', Wk, x) + bk[None, :, None]
            v = jnp.einsum('oc,bcl->bol', Wv, x) + bv[None, :, None]
            energy = jnp.einsum('bci,bcj->bij', q, k)
            attn = jax.nn.softmax(energy, axis=-1)
            out = jnp.einsum('bcj,bij->bci', v, attn)
            return gamma * out + x
        B, D = x.shape
        emb_sample, emb_task = (x[:, :D // 2], x[:, D // 2:])
        h = jnp.stack([emb_sample, emb_task], axis=1)
        h = _maxpool(jax.nn.relu(_bn(_conv1d(h, w1, b1, 1, 1), g1, be1, m1, v1)), 8)
        h = _maxpool(jax.nn.relu(_bn(_conv1d(h, w2, b2, 1, 1), g2, be2, m2, v2)), 4)
        h = _self_attn(h, wq, bq, wk, bk, wv, bv, gamma)
        h = _bn(_conv1d(h, w3, b3, 2, 1), g3, be3, m3, v3)
        return h

    def _L0_attn_ref(x, kln_weight, kln_bias, vln_weight, vln_bias):
        import jax, jax.numpy as jnp
        import numpy as np
        HEADS = 8
        EPS = 1e-05

        def _ln(t, w, b, headc):
            m = jnp.mean(t, axis=-1, keepdims=True)
            d = t - m
            std = jnp.sqrt(jnp.sum(d * d, axis=-1, keepdims=True) / (headc - 1))
            return w * (d / (std + EPS)) + b
        B, N, C = x.shape
        headc = C // HEADS
        qkv = x.reshape(B, N, HEADS, headc).transpose(0, 2, 1, 3)
        k = _ln(qkv, kln_weight, kln_bias, headc)
        v = _ln(qkv, vln_weight, vln_bias, headc)
        kv = jnp.einsum('bhnd,bhne->bhde', k, v) / N
        out = jnp.einsum('bhnd,bhde->bhne', qkv, kv)
        out = out.transpose(0, 2, 1, 3).reshape(B, N, C)
        return out + x

    def _L0_ffn_ref(x, ln1_w, ln2_w, wq, wk, wv, wo, router_w, w1, w2, w3):
        import jax, jax.numpy as jnp
        import numpy as np
        B, T, C = (64, 96, 64)
        NH, NKV = (4, 2)
        HD = C // NH
        NREP = NH // NKV
        NE, TOPK = (8, 2)
        HID = int(8 / 3 * C)
        EPS_RMS = 1e-06

        def _rope_tables(t_len):
            inv_freq = 1.0 / 10000.0 ** (np.arange(0, HD, 2, dtype=np.float32) / HD)
            t = np.arange(t_len, dtype=np.float32)
            freqs = np.outer(t, inv_freq)
            emb = np.concatenate([freqs, freqs], axis=-1)
            return (jnp.asarray(np.cos(emb)), jnp.asarray(np.sin(emb)))

        def _rotate_half(x):
            h = x.shape[-1] // 2
            return jnp.concatenate([-x[..., h:], x[..., :h]], axis=-1)

        def _rmsnorm(v, w):
            return v * jax.lax.rsqrt(jnp.mean(v * v, axis=-1, keepdims=True) + EPS_RMS) * w
        Bx, Tx, Cx = x.shape
        h = _rmsnorm(x, ln1_w)
        q = (h @ wq.T).reshape(Bx, Tx, NH, HD).transpose(0, 2, 1, 3)
        k = (h @ wk.T).reshape(Bx, Tx, NKV, HD).transpose(0, 2, 1, 3)
        v = (h @ wv.T).reshape(Bx, Tx, NKV, HD).transpose(0, 2, 1, 3)
        cos, sin = _rope_tables(Tx)
        cos, sin = (cos[None, None], sin[None, None])
        q = q * cos + _rotate_half(q) * sin
        k = k * cos + _rotate_half(k) * sin
        k = jnp.repeat(k, NREP, axis=1)
        v = jnp.repeat(v, NREP, axis=1)
        scores = jnp.einsum('bhtd,bhsd->bhts', q, k) / jnp.sqrt(jnp.float32(HD))
        causal = jnp.tril(jnp.ones((Tx, Tx), dtype=bool))
        scores = jnp.where(causal[None, None], scores, jnp.float32(-1e+30))
        att = jax.nn.softmax(scores, axis=-1)
        y = jnp.einsum('bhts,bhsd->bhtd', att, v).transpose(0, 2, 1, 3).reshape(Bx, Tx, Cx)
        x = x + y @ wo.T
        flat = _rmsnorm(x, ln2_w).reshape(-1, Cx)
        probs = jax.nn.softmax(flat @ router_w.T, axis=-1)
        tp, ti = jax.lax.top_k(probs, TOPK)
        tp = tp / (jnp.sum(tp, axis=-1, keepdims=True) + 1e-09)
        weights = jnp.sum(tp[..., None] * jax.nn.one_hot(ti, NE, dtype=flat.dtype), axis=1)
        out = jnp.zeros_like(flat)
        for e in range(NE):
            hh = jax.nn.silu(flat @ w1[e].T) * (flat @ w3[e].T)
            out = out + weights[:, e:e + 1] * (hh @ w2[e].T)
        return x + out.reshape(Bx, Tx, Cx)

    def _L1_attn_ref(x, Wq, Wk, Wv, Wo):
        import jax, jax.numpy as jnp
        import numpy as np
        B, L, D = (4, 1024, 64)
        q = x @ Wq.T
        k = x @ Wk.T
        v = x @ Wv.T
        logits = jnp.einsum('bld,bmd->blm', q, k)
        Lq = x.shape[1]
        causal_mask = jnp.triu(jnp.ones((Lq, Lq), dtype=bool), k=1)
        logits = jnp.where(causal_mask[None], jnp.asarray(0.0, logits.dtype), logits)
        attn = jax.nn.relu(logits)
        row_counts = jnp.maximum(jnp.arange(Lq, dtype=attn.dtype), 1.0)
        attn = attn / row_counts[None, :, None]
        ctx = jnp.einsum('blm,bmd->bld', attn, v)
        return ctx @ Wo.T

    def _L1_ffn_ref(input_embeddings, router_w, w1, b1, w2, b2):
        import jax, jax.numpy as jnp
        import numpy as np
        NUM_EXPERTS = 8
        TOP_K = 2
        B, S, D = (8, 2048, 64)

        def _moe(tokens, router_w, w1, b1, w2, b2):
            N = tokens.shape[0]
            E = router_w.shape[0]
            logits = tokens.astype(jnp.float32) @ router_w.astype(jnp.float32).T
            probs = jax.nn.softmax(logits, axis=-1)
            rw, re = jax.lax.top_k(probs, TOP_K)
            if TOP_K > 1:
                rw = rw / jnp.maximum(rw.sum(-1, keepdims=True), 1e-12)
            rw = rw.astype(tokens.dtype)
            combine = jnp.zeros((N, E), tokens.dtype).at[jnp.arange(N)[:, None], re].set(rw)
            out = tokens
            for e in range(E):
                h = jax.nn.gelu(tokens @ w1[e] + b1[e], approximate=False)
                y = h @ w2[e] + b2[e]
                out = out + combine[:, e:e + 1] * y
            return out
        b, s, d = input_embeddings.shape
        tokens = input_embeddings.reshape(b * s, d)
        return _moe(tokens, router_w, w1, b1, w2, b2).reshape(b, s, d)
    h = _L0_tok_ref(x, L0_tok_w1, L0_tok_b1, L0_tok_g1, L0_tok_be1, L0_tok_m1, L0_tok_v1, L0_tok_w2, L0_tok_b2, L0_tok_g2, L0_tok_be2, L0_tok_m2, L0_tok_v2, L0_tok_wq, L0_tok_bq, L0_tok_wk, L0_tok_bk, L0_tok_wv, L0_tok_bv, L0_tok_gamma, L0_tok_w3, L0_tok_b3, L0_tok_g3, L0_tok_be3, L0_tok_m3, L0_tok_v3)
    h = h + _L0_attn_ref(_layernorm(h, axis=-1), L0_attn_kln_weight, L0_attn_kln_bias, L0_attn_vln_weight, L0_attn_vln_bias)
    h = h + _L0_ffn_ref(_layernorm(h, axis=-1), L0_ffn_ln1_w, L0_ffn_ln2_w, L0_ffn_wq, L0_ffn_wk, L0_ffn_wv, L0_ffn_wo, L0_ffn_router_w, L0_ffn_w1, L0_ffn_w2, L0_ffn_w3)
    h = h + _L1_attn_ref(_layernorm(h, axis=-1), L1_attn_Wq, L1_attn_Wk, L1_attn_Wv, L1_attn_Wo)
    h = h + _L1_ffn_ref(_layernorm(h, axis=-1), L1_ffn_router_w, L1_ffn_w1, L1_ffn_b1, L1_ffn_w2, L1_ffn_b2)
    return h

_drawn_inputs = setup_inputs


def setup_inputs(seed=0):
    import zlib

    import numpy as np

    out = dict(_drawn_inputs(seed))
    spreads = {'L0_attn_kln_weight': (1.0, 0.2),
     'L0_attn_kln_bias': (0.0, 0.538),
     'L0_attn_vln_weight': (1.0, 0.2),
     'L0_attn_vln_bias': (0.0, 0.496),
     'L0_ffn_ln1_w': (1.0, 0.6),
     'L0_ffn_ln2_w': (1.0, 0.6),
     'L1_ffn_b1': (0.0, 0.8),
     'L1_ffn_b2': (0.0, 0.514)}
    factors = {'L0_tok_wq': 8.0,
     'L0_tok_bq': 8.0,
     'L0_tok_wk': 8.0,
     'L0_tok_bk': 8.0,
     'L0_tok_b3': 2.844,
     'L0_tok_g3': 4.774,
     'L0_tok_be3': 3.274,
     'L0_tok_v3': 3.344,
     'L0_ffn_wq': 8.0,
     'L0_ffn_wk': 8.0,
     'L0_ffn_wv': 8.0,
     'L0_ffn_wo': 8.0,
     'L0_ffn_router_w': 8.0,
     'L0_ffn_w1': 8.0,
     'L0_ffn_w2': 8.0,
     'L0_ffn_w3': 8.0,
     'L1_attn_Wq': 8.0,
     'L1_attn_Wk': 8.0,
     'L1_attn_Wv': 8.0,
     'L1_attn_Wo': 8.0}
    for name, (base, spread) in spreads.items():
        noise = np.random.default_rng([zlib.crc32(name.encode()), seed]).standard_normal(out[name].shape)
        drawn = base * np.exp(spread * noise) if base else spread * noise
        out[name] = jnp.asarray(drawn.astype(out[name].dtype))
    for name, factor in factors.items():
        out[name] = (out[name] * factor).astype(out[name].dtype)
    return out
```

```python
from contextlib import ExitStack

import numpy as np

import concourse.bass as bass
from concourse import mybir

F32 = mybir.dt.float32
BF16 = mybir.dt.bfloat16
F32R = mybir.dt.float32r
ALU = mybir.AluOpType
ACT = mybir.ActivationFunctionType
AX = mybir.AxisListType.X

B, D_IN = 64, 8192
NT, C = 128, 64
HALF = D_IN // 2
GB = 8
NG = B // GB
PR = GB // 2
C1, C2, CQ = 16, 64, 8
L1, L2 = HALF // 8, HALF // 32
HC = 8
NH, NKV, HD = 4, 2, 16
NE = 8
HID = int(8 / 3 * C)
REM = HID - 128
RT = 3
NJ = NE + -(-NE // RT)
EPS = 1e-05
EPS_RMS = 1e-06

PACKS = {
    "tok": [("w1t", 128), ("g1row", 128), ("v1row", 128), ("w2t", 3 * 128), ("g2row", 128), ("v2row", 128),
            ("wq", 64), ("wk", 64), ("wv", 128), ("w3t", 4 * 128),
            ("cb", 3), ("cg", 3), ("cbe", 3), ("cm", 3), ("cv", 3), ("bq", 1), ("bk", 1), ("bv", 1), ("gamma", 1)],
    "const": [("ident", 128), ("headmask", 128), ("causal", 128), ("cosq", NT), ("sinq", NT), ("cosk", NT),
              ("sink", NT), ("hsel", NH), ("rev", NE), ("relumask", NT)],
    "att": [("kw", C), ("kb", C), ("vw", C), ("vb", C), ("ln1", 1), ("ln2", 1),
            ("fwq", 128), ("fwqr", 128), ("fwk", 128), ("fwkr", 128), ("fwv", 64), ("fwo", 128), ("frouter", NE),
            ("awq", 128), ("awk", 128), ("awv", 128), ("awo", 128), ("grouter", NE), ("gb1", 4), ("gb2", GB * C)],
    "moe0": [("w13", NJ * 2 * 128), ("w2", NE * C), ("w2r", (NJ - NE) * RT * C)],
    "moe1": [("gw1", 4 * 128), ("gw2", 4 * 128)],
}


def width(pack):
    return sum(n for _, n in PACKS[pack])


class SEMS:

    ctx = None


class Steps:

    def __init__(self, eng, sem, n):
        self.eng, self.sem, self.n = eng, sem, n

    def begin(self, i):
        self.base, self.k = i * self.n, 0

    def __call__(self, ins):
        self.k += 1
        ins.then_inc(self.sem, 1)
        self.eng.wait_ge(self.sem, self.base + self.k)

    def end(self):
        assert self.k == self.n, self.k


def build(nc, x, tok, const, att, moe0, moe1, out, stop_after=9):
    ctx = ExitStack()
    with ctx:
        def sb(name, shape, dt=F32):
            return ctx.enter_context(nc.sbuf_tensor(name, shape, dt))

        def sem(name):
            return ctx.enter_context(nc.semaphore(name))

        SEMS.ctx = ctx
        PS = ctx.enter_context(nc.psum_tensor("PS", [128, 8, 512], F32))
        W = {}
        landed = {}
        packs = {}
        for name, src in (("tok", tok), ("const", const), ("att", att), ("moe0", moe0), ("moe1", moe1)):
            t = sb(f"pack_{name}", [128, width(name)])
            landed[name] = sem(f"landed_{name}") if name in ("tok", "const") else landed.get("att") or sem("landed_rest")
            packs[name] = (t, src)
            at = 0
            for part, n in PACKS[name]:
                W[part] = t[:, at:at + n]
                at += n
        H = sb("H", [128, B, C])
        FT = sb("FT", [128, B, NT])
        WT = sb("WT", [128, B, NE])
        neg_half = sb("neg_half", [128, 1])
        half = sb("half", [128, 1])

        phase_tokenizer(nc, x, packs, landed, W, PS, H, neg_half, half)
        if stop_after >= 2:
            phase_head_attention(nc, W, PS, H, neg_half, half)
        if stop_after >= 3:
            phase_causal_attention(nc, W, PS, H, FT, WT, neg_half)
        if stop_after >= 4:
            phase_swiglu_experts(nc, W, PS, H, FT, WT)
        if stop_after >= 5:
            phase_relu_attention(nc, W, PS, H, FT, WT, neg_half)
        if stop_after >= 6:
            phase_gelu_experts(nc, W, PS, H, FT, WT, out)
        else:
            phase_dump(nc, H, out)


def phase_tokenizer(nc, x, packs, landed, W, PS, H, neg_half, half):
    ctx = ExitStack()
    with ctx:
        def sb(name, shape, dt=F32):
            return ctx.enter_context(nc.sbuf_tensor(name, shape, dt))

        def sem(name):
            return SEMS.ctx.enter_context(nc.semaphore(name))

        QL = HALF // 2
        xs = sb("xs", [112, QL])
        w1s = sb("w1s", [112, 128])
        w2s = sb("w2s", [128, 3, 128])
        srow = sb("srow", [128, 2, 128])
        scol = sb("scol", [128, 3])
        tcol = sb("tcol", [128, 3])
        wvg = sb("wvg", [128, 128])
        bvg = sb("bvg", [128, 1])
        h1raw = sb("h1raw", [128, L1])
        h1 = sb("h1", [128, L1 + 2])
        h2raw = sb("h2raw", [128, PR, L2])
        h2 = sb("h2", [128, PR, L2])
        qs = sb("qs", [64, PR, L2])
        ks = sb("ks", [64, PR, L2])
        vT = sb("vT", [128, PR, 128])
        nmax = sb("nmax", [128, GB])
        rowsum = sb("rowsum", [128, GB])
        rinv = sb("rinv", [128, GB])
        pexp = sb("pexp", [128, GB, 128])
        pnorm = sb("pnorm", [128, GB, 128])
        pT = sb("pT", [128, GB, 128])
        ha = sb("ha", [128, PR, L2 + 2])

        s_const = sem("s_const")
        s_rows = sem("s_rows")
        s_pow = sem("s_pow")
        s_fold = sem("s_fold")
        s_wready = sem("s_wready")
        x_in = sem("x_in")
        conv1_mm = sem("conv1_mm")
        conv1_pooled = sem("conv1_pooled")
        h1_ready = sem("h1_ready")
        conv2_mm = sem("conv2_mm")
        conv2_pooled = sem("conv2_pooled")
        h2_ready = sem("h2_ready")
        qkv_mm = sem("qkv_mm")
        qk_ready = sem("qk_ready")
        v_ready = sem("v_ready")
        energy_mm = sem("energy_mm")
        max_ready = sem("max_ready")
        exp_ready = sem("exp_ready")
        pnorm_ready = sem("pnorm_ready")
        pT_mm = sem("pT_mm")
        pT_act = sem("pT_act")
        pT_dve = sem("pT_dve")
        av_mm = sem("av_mm")
        ha_ready = sem("ha_ready")
        conv3_mm = sem("conv3_mm")
        h_written = sem("h_written")
        block = ctx.enter_context(nc.Block())
        NB = 8
        xrow = x.rearrange("b (c l) -> (b c) l", c=2)

        @block.sync
        def _(sp):
            for name in ("tok", "const", "att", "moe0", "moe1"):
                t, src = packs[name]
                sp.dma_start(t[:, :], src).then_inc(landed[name], 16)
            sp.wait_ge(s_const, 2)
            with sp.Fori(0, NG) as i:
                sp.wait_ge(conv1_mm, i * NB)
                for hf in range(2):
                    for tap in range(3):
                        lo = 1 if (hf, tap) == (0, 0) else 0
                        hi = QL - 1 if (hf, tap) == (1, 2) else QL
                        at = hf * QL + tap - 1
                        row = 64 * hf + 16 * tap
                        sp.dma_start(xs[row:row + 16, lo:hi], xrow[bass.ds(i * 16, 16), at + lo:at + hi])\
                            .then_inc(x_in, 16)
            sp.wait_ge(landed["att"], 48)

        @block.gpsimd
        def _(pool):
            nc.gpsimd.memset(neg_half[:, :], -0.5).then_inc(s_const, 1)
            pool.wait_ge(s_const, 1)
            nc.gpsimd.memset(half[:, :], 0.5).then_inc(s_rows, 1)
            pool.wait_ge(s_rows, 4)
            nc.gpsimd.tensor_tensor(srow[:, :, :], srow[:, :, :],
                                    neg_half[:, :].unsqueeze(2).broadcast_to([128, 2, 128]), ALU.pow).then_inc(s_pow, 1)
            nc.gpsimd.tensor_tensor(scol[:, :], scol[:, :],
                                    neg_half[:, :].broadcast_to([128, 3]), ALU.pow).then_inc(s_pow, 1)

        @block.tensor
        def _(pe):
            def conv1(i):
                pe.wait_ge(x_in, i * 96 + 96)
                for c in range(NB // 2):
                    for hf in range(2):
                        u = 2 * c + hf
                        if u >= 4:
                            pe.wait_ge(conv1_pooled, i * NB + u - 3)
                        lo = 64 * hf
                        nc.tensor.matmul(PS[:, u % 4, :], w1s[lo:lo + 48, :], xs[lo:lo + 48, c * 512:(c + 1) * 512],
                                         start=True, stop=True).then_inc(conv1_mm, 1)

            def conv2(i):
                pe.wait_ge(h1_ready, i + 1)
                for tap in range(3):
                    for p in range(PR):
                        mm = nc.tensor.matmul(PS[:, 4 + p, :], w2s[32 * p:32 * p + 32, tap, :],
                                              h1[32 * p:32 * p + 32, tap:tap + L1],
                                              start=(tap == 0), stop=(tap == 2))
                        if tap == 2:
                            mm.then_inc(conv2_mm, 1)

            def attention(i):
                pe.wait_ge(h2_ready, i + 1)
                nc.tensor.matmul(PS[0:64, 0, :], W["wq"], h2[:, :, :], start=True, stop=True).then_inc(qkv_mm, 1)
                nc.tensor.matmul(PS[0:64, 1, :], W["wk"], h2[:, :, :], start=True, stop=True).then_inc(qkv_mm, 1)
                for p in range(PR):
                    mm = nc.tensor.matmul(PS[:, 2, p * 128:(p + 1) * 128], h2[:, p, :], wvg[:, :],
                                          start=True, stop=True)
                mm.then_inc(qkv_mm, 1)
                pe.wait_ge(qk_ready, i * 2 + 2)
                for p in range(PR):
                    for hf in range(2):
                        r = slice(32 * hf, 32 * hf + 32)
                        mm = nc.tensor.matmul(PS[:, 4 + hf, p * 128:(p + 1) * 128], qs[r, p, :], ks[r, p, :],
                                              start=True, stop=True)
                        if p == PR - 1:
                            mm.then_inc(energy_mm, 1)
                pe.wait_ge(pnorm_ready, i * 2 + 2)
                for hf in range(2):
                    for p in range(PR):
                        mm = nc.tensor.transpose(PS[:, 6 + hf, p * 128:(p + 1) * 128],
                                                 pnorm[:, hf * PR + p, :], W["ident"])
                    mm.then_inc(pT_mm, 1)
                pe.wait_ge(v_ready, i + 1)
                pe.wait_ge(pT_act, i + 1)
                pe.wait_ge(pT_dve, i + 1)
                for p in range(PR):
                    for hf in range(2):
                        mm = nc.tensor.matmul(PS[64 * hf:64 * hf + 64, 3, p * 128:(p + 1) * 128],
                                              vT[:, p, 64 * hf:64 * hf + 64], pT[:, hf * PR + p, :],
                                              start=True, stop=True)
                mm.then_inc(av_mm, 1)
                pe.wait_ge(ha_ready, i + 1)
                for tap in range(4):
                    for hf in range(2):
                        r = slice(64 * hf, 64 * hf + 64)
                        mm = nc.tensor.matmul(PS[:, hf, 0:PR * C], W["w3t"][r, tap * 128:(tap + 1) * 128],
                                              ha[r, :, tap:tap + 2 * C - 1:2],
                                              start=(tap == 0), stop=(tap == 3))
                        if tap == 3:
                            mm.then_inc(conv3_mm, 1)

            pe.wait_ge(landed["const"], 16)
            pe.wait_ge(s_wready, 1)
            with pe.Fori(0, NG) as i:
                pe.wait_ge(h_written, i * 2)
                conv1(i)
                conv2(i)
                attention(i)

        @block.scalar
        def _(act):
            act.wait_ge(s_wready, 1)
            with act.Fori(0, NG) as i:
                act.wait_ge(conv1_pooled, i * NB + NB)
                act.wait_ge(conv2_mm, i * PR)
                nc.scalar.activation(h1[:, 1:L1 + 1], h1raw[:, :], ACT.Relu, bias=tcol[:, 0:1]).then_inc(h1_ready, 1)
                act.wait_ge(conv2_pooled, i * PR + PR)
                act.wait_ge(ha_ready, i)
                nc.scalar.activation(h2[:, :, :], h2raw[:, :, :], ACT.Relu, bias=tcol[:, 1:2]).then_inc(h2_ready, 1)
                act.wait_ge(qkv_mm, i * 3 + 1)
                nc.scalar.activation(qs[:, :, :], PS[0:64, 0, :].rearrange("p (a b) -> p a b", a=PR), ACT.Identity,
                                     bias=W["bq"][0:64]).then_inc(qk_ready, 1)
                act.wait_ge(qkv_mm, i * 3 + 2)
                nc.scalar.activation(ks[:, :, :], PS[0:64, 1, :].rearrange("p (a b) -> p a b", a=PR), ACT.Identity,
                                     bias=W["bk"][0:64]).then_inc(qk_ready, 1)
                for hf in range(2):
                    act.wait_ge(max_ready, i * 2 + hf + 1)
                    for p in range(PR):
                        u = hf * PR + p
                        nc.scalar.activation(pexp[:, u, :], PS[:, 4 + hf, p * 128:(p + 1) * 128], ACT.Exp,
                                             bias=nmax[:, u:u + 1], accum_out=rowsum[:, u:u + 1])\
                            .then_inc(exp_ready, 1)
                act.wait_ge(pT_mm, i * 2 + 1)
                nc.scalar.activation(pT[:, 0:PR, :], PS[:, 6, :].rearrange("p (a b) -> p a b", a=PR), ACT.Copy)\
                    .then_inc(pT_act, 1)
                for hf in range(2):
                    act.wait_ge(conv3_mm, i * 2 + hf + 1)
                    dst = H[:, bass.ds(i * GB, GB), :].rearrange("n (p f) t -> n p f t", f=2)[:, :, hf, :]
                    nc.scalar.activation(dst, PS[:, hf, 0:PR * C].rearrange("n (p t) -> n p t", p=PR), ACT.Identity,
                                         bias=tcol[:, 2:3], scale=scol[:, 2:3]).then_inc(h_written, 1)
            act.wait_ge(h_written, NG * 2)

        @block.vector
        def _(dve):
            dve.wait_ge(s_const, 1)
            nc.vector.memset(xs[0:16, 0:1], 0.0).then_inc(s_rows, 1)
            dve.wait_ge(s_rows, 2)
            nc.vector.memset(xs[96:112, QL - 1:QL], 0.0).then_inc(s_const, 1)
            nc.vector.memset(h1[:, 0:L1 + 2:L1 + 1], 0.0)
            nc.vector.memset(ha[:, :, 0:L2 + 2:L2 + 1], 0.0)
            dve.wait_ge(landed["tok"], 16)
            nc.vector.tensor_scalar_add(srow[:, 0, :], W["v1row"], EPS)
            nc.vector.tensor_scalar_add(srow[:, 1, :], W["v2row"], EPS).then_inc(s_rows, 1)
            nc.vector.tensor_scalar_add(scol[:, :], W["cv"], EPS).then_inc(s_rows, 1)
            dve.wait_ge(s_pow, 2)
            fold = Steps(dve, s_fold, 8)
            fold.begin(0)
            fold(nc.vector.tensor_tensor(srow[:, 0, :], srow[:, 0, :], W["g1row"], ALU.mult))
            fold(nc.vector.tensor_tensor(srow[:, 1, :], srow[:, 1, :], W["g2row"], ALU.mult))
            fold(nc.vector.tensor_tensor(scol[:, :], scol[:, :], W["cg"], ALU.mult))
            fold(nc.vector.tensor_tensor(tcol[:, :], W["cb"], W["cm"], ALU.subtract))
            fold(nc.vector.tensor_tensor(tcol[:, :], tcol[:, :], scol[:, :], ALU.mult))
            fold(nc.vector.tensor_tensor(tcol[:, :], tcol[:, :], W["cbe"], ALU.add))
            nc.vector.tensor_tensor(w1s[0:64, :], W["w1t"][0:64], srow[0:64, 0, :], ALU.mult)
            fold(nc.vector.tensor_tensor(w1s[64:112, :], W["w1t"][64:112], srow[64:112, 0, :], ALU.mult))
            nc.vector.tensor_tensor(w2s[:, :, :], W["w2t"].rearrange("p (t m) -> p t m", t=3),
                                    srow[:, 1, :].unsqueeze(1).broadcast_to([128, 3, 128]), ALU.mult)
            nc.vector.tensor_scalar(bvg[:, :], W["bv"], W["gamma"], None, ALU.mult)
            fold(nc.vector.tensor_scalar(wvg[:, :], W["wv"], W["gamma"], None, ALU.mult))
            fold.end()
            nc.vector.tensor_copy(rinv[:, 0:1], scol[:, 0:1]).then_inc(s_wready, 1)
            with dve.Fori(0, NG) as i:
                dve.wait_ge(h1_ready, i)
                for u in range(NB):
                    dve.wait_ge(conv1_mm, i * NB + u + 1)
                    at = (u % 2) * 4 + u // 2
                    nc.vector.tensor_reduce(out=h1raw[:, at * 64:(at + 1) * 64],
                                            in_=PS[:, u % 4, :].rearrange("p (a b) -> p a b", b=8),
                                            axis=AX, op=ALU.max).then_inc(conv1_pooled, 1)
                dve.wait_ge(h2_ready, i)
                for p in range(PR):
                    dve.wait_ge(conv2_mm, i * PR + p + 1)
                    nc.vector.tensor_reduce(out=h2raw[:, p, :], in_=PS[:, 4 + p, :].rearrange("p (a b) -> p a b", b=4),
                                            axis=AX, op=ALU.max).then_inc(conv2_pooled, 1)
                dve.wait_ge(qkv_mm, i * 3 + 3)
                nc.vector.tensor_copy(vT[:, :, :], PS[:, 2, :].rearrange("p (a b) -> p a b", a=PR)).then_inc(v_ready, 1)
                for hf in range(2):
                    dve.wait_ge(energy_mm, i * 2 + hf + 1)
                    nc.vector.tensor_reduce(out=nmax[:, hf * PR:(hf + 1) * PR],
                                            in_=PS[:, 4 + hf, :].rearrange("p (a b) -> p a b", a=PR),
                                            axis=AX, op=ALU.max, negate=True).then_inc(max_ready, 1)
                dve.wait_ge(exp_ready, i * GB + GB)
                nc.vector.reciprocal(rinv[:, :], rowsum[:, :]).then_inc(pnorm_ready, 1)
                dve.wait_ge(pnorm_ready, i * 2 + 1)
                nc.vector.tensor_tensor(pnorm[:, :, :], pexp[:, :, :],
                                        rinv[:, :].unsqueeze(2).broadcast_to([128, GB, 128]), ALU.mult)\
                    .then_inc(pnorm_ready, 1)
                dve.wait_ge(pT_mm, i * 2 + 2)
                nc.vector.tensor_copy(pT[:, PR:GB, :], PS[:, 7, :].rearrange("p (a b) -> p a b", a=PR))\
                    .then_inc(pT_dve, 1)
                dve.wait_ge(av_mm, i + 1)
                nc.vector.scalar_tensor_tensor(out=ha[:, :, 1:L2 + 1],
                                               in0=PS[:, 3, :].rearrange("p (a b) -> p a b", a=PR),
                                               scalar=bvg[:, 0:1], in1=h2[:, :, :],
                                               op0=ALU.add, op1=ALU.add).then_inc(ha_ready, 1)


class LayerNorm:

    def __init__(self, nc, ctx, tag, neg_half):
        self.nc, self.neg_half = nc, neg_half

        def sb(name, shape):
            return ctx.enter_context(nc.sbuf_tensor(f"{tag}_{name}", shape, F32))

        def sem(name):
            return SEMS.ctx.enter_context(nc.semaphore(f"{tag}_{name}"))

        self.mean = sb("mean", [128, GB])
        self.dev = sb("dev", [128, GB, C])
        self.sq = sb("sq", [128, GB, C])
        self.var = sb("var", [128, GB])
        self.rstd = sb("rstd", [128, GB])
        self.s_steps = sem("steps")
        self.s_dev = sem("dev_ready")
        self.s_sq = sem("sq_ready")
        self.s_var = sem("var_ready")
        self.s_rstd = sem("rstd_ready")

    def vector(self, dve, i, src, dst):
        nc = self.nc
        step = Steps(dve, self.s_steps, 3)
        step.begin(i)
        step(nc.vector.tensor_reduce(out=self.mean[:, :], in_=src, axis=AX, op=ALU.add))
        step(nc.vector.tensor_scalar_mul(self.mean[:, :], self.mean[:, :], 1.0 / C))
        nc.vector.tensor_tensor(self.dev[:, :, :], src, self.mean[:, :].unsqueeze(2).broadcast_to([128, GB, C]),
                                ALU.subtract).then_inc(self.s_dev, 1)
        dve.wait_ge(self.s_sq, i + 1)
        step(nc.vector.tensor_reduce(out=self.var[:, :], in_=self.sq[:, :, :], axis=AX, op=ALU.add))
        step.end()
        nc.vector.tensor_scalar(self.var[:, :], self.var[:, :], 1.0 / C, EPS, ALU.mult, ALU.add)\
            .then_inc(self.s_var, 1)
        dve.wait_ge(self.s_rstd, i + 1)
        return nc.vector.tensor_tensor(dst, self.dev[:, :, :],
                                       self.rstd[:, :].unsqueeze(2).broadcast_to([128, GB, C]), ALU.mult)

    def scalar(self, act, i):
        act.wait_ge(self.s_dev, i + 1)
        self.nc.scalar.activation(self.sq[:, :, :], self.dev[:, :, :], ACT.Square).then_inc(self.s_sq, 1)

    def gpsimd(self, pool, i):
        pool.wait_ge(self.s_var, i + 1)
        self.nc.gpsimd.tensor_tensor(self.rstd[:, :], self.var[:, :], self.neg_half[:, :].broadcast_to([128, GB]),
                                     ALU.pow).then_inc(self.s_rstd, 1)


class RmsNorm:

    def __init__(self, nc, ctx, tag, neg_half):
        self.nc, self.neg_half = nc, neg_half

        def sb(name, shape):
            return ctx.enter_context(nc.sbuf_tensor(f"{tag}_{name}", shape, F32))

        def sem(name):
            return SEMS.ctx.enter_context(nc.semaphore(f"{tag}_{name}"))

        self.sq = sb("sq", [128, GB, C])
        self.ms = sb("ms", [128, GB])
        self.rstd = sb("rstd", [128, GB])
        self.s_sq = sem("sq_ready")
        self.s_ms = sem("ms_ready")
        self.s_rstd = sem("rstd_ready")

    def vector(self, dve, i, src, dst):
        nc = self.nc
        dve.wait_ge(self.s_sq, i + 1)
        nc.vector.tensor_reduce(out=self.ms[:, :], in_=self.sq[:, :, :], axis=AX, op=ALU.add).then_inc(self.s_ms, 1)
        dve.wait_ge(self.s_ms, i * 2 + 1)
        nc.vector.tensor_scalar(self.ms[:, :], self.ms[:, :], 1.0 / C, EPS_RMS, ALU.mult, ALU.add)\
            .then_inc(self.s_ms, 1)
        dve.wait_ge(self.s_rstd, i + 1)
        return nc.vector.tensor_tensor(dst, src, self.rstd[:, :].unsqueeze(2).broadcast_to([128, GB, C]), ALU.mult)

    def scalar(self, act, i, src):
        self.nc.scalar.activation(self.sq[:, :, :], src, ACT.Square).then_inc(self.s_sq, 1)

    def gpsimd(self, pool, i):
        pool.wait_ge(self.s_ms, i * 2 + 2)
        self.nc.gpsimd.tensor_tensor(self.rstd[:, :], self.ms[:, :], self.neg_half[:, :].broadcast_to([128, GB]),
                                     ALU.pow).then_inc(self.s_rstd, 1)


class TopTwo:

    STEPS = 17

    def __init__(self, nc, ctx, tag, rev, floor, op):
        self.nc, self.rev, self.floor, self.op = nc, rev, floor, op

        def sb(name, shape):
            return ctx.enter_context(nc.sbuf_tensor(f"{tag}_{name}", shape, F32))

        def sem(name):
            return SEMS.ctx.enter_context(nc.semaphore(f"{tag}_{name}"))

        self.col = [sb(f"col{n}", [128, GB]) for n in range(5)]
        self.mat = [sb(f"mat{n}", [128, GB, NE]) for n in range(5)]
        self.ex = sb("ex", [128, GB, NE])
        self.s_steps = sem("steps")
        self.s_shift = sem("shifted")
        self.s_exp = sem("exp_ready")

    def vector(self, dve, i, logits, dst):
        nc, V = self.nc, self.nc.vector
        m1, den, p1, p2, kmax = (c[:, :] for c in self.col)
        lg, p, key, oh1, oh2 = (m[:, :, :] for m in self.mat)
        ex = self.ex[:, :, :]

        def wide(c):
            return c.unsqueeze(2).broadcast_to([128, GB, NE])

        rev = self.rev.unsqueeze(1).broadcast_to([128, GB, NE])
        step = Steps(dve, self.s_steps, self.STEPS)
        step.begin(i)
        step(V.tensor_reduce(out=m1, in_=logits, axis=AX, op=ALU.max))
        V.tensor_tensor(lg, logits, wide(m1), ALU.subtract).then_inc(self.s_shift, 1)
        dve.wait_ge(self.s_exp, i + 1)
        step(V.tensor_reduce(out=den, in_=ex, axis=AX, op=ALU.add))
        step(V.reciprocal(den, den))
        step(V.tensor_tensor(p, ex, wide(den), ALU.mult))

        def first_of_largest(src, largest, one_hot):
            step(V.tensor_reduce(out=largest, in_=src, axis=AX, op=ALU.max))
            step(V.tensor_tensor(key, src, wide(largest), ALU.is_equal))
            step(V.tensor_tensor(key, key, rev, ALU.mult))
            step(V.tensor_reduce(out=kmax, in_=key, axis=AX, op=ALU.max))
            return V.tensor_tensor(one_hot, key, wide(kmax), ALU.is_equal)

        step(first_of_largest(p, p1, oh1))
        step(V.scalar_tensor_tensor(out=lg, in0=oh1, scalar=-2.0, in1=p, op0=ALU.mult, op1=ALU.add))
        first_of_largest(lg, p2, oh2)
        V.tensor_tensor(den, p1, p2, ALU.add)
        step(V.tensor_copy(m1, p1))
        V.tensor_scalar(den, den, self.floor, None, self.op)
        step(V.tensor_tensor(oh1, oh1, oh2, ALU.add))
        V.reciprocal(den, den)
        step(V.tensor_tensor(p, p, oh1, ALU.mult))
        step.end()
        return V.tensor_tensor(dst, p, wide(den), ALU.mult)

    def scalar(self, act, i):
        act.wait_ge(self.s_shift, i + 1)
        self.nc.scalar.activation(self.ex[:, :, :], self.mat[0][:, :, :], ACT.Exp).then_inc(self.s_exp, 1)


def group(t, i):
    return t[:, bass.ds(i * GB, GB), :]


def pairs(bank):
    return bank.rearrange("p (a b) -> p a b", a=PR)


def seqs(bank):
    return bank.rearrange("p (a b) -> p a b", a=GB)


def two(t, p):
    return t[:, 2 * p:2 * p + 2, :].rearrange("p a b -> p (a b)")


def phase_head_attention(nc, W, PS, H, neg_half, half):
    ctx = ExitStack()
    with ctx:
        def sb(name, shape, dt=F32):
            return ctx.enter_context(nc.sbuf_tensor(name, shape, dt))

        def sem(name):
            return SEMS.ctx.enter_context(nc.semaphore(name))

        NHD = GB * C // HC
        ln = LayerNorm(nc, ctx, "hln", neg_half)
        z = sb("b_z", [128, GB, C])
        hmean = sb("hmean", [128, NHD])
        hdev = sb("hdev", [128, NHD, HC])
        hsq = sb("hsq", [128, NHD, HC])
        hvar = sb("hvar", [128, NHD])
        hstd = sb("hstd", [128, NHD])
        hn = sb("hn", [128, GB, C])
        kt = sb("kt", [128, GB, C])
        vt = sb("vt", [128, GB, C])
        zT = sb("b_zT", [128, PR, NT])
        kvm = sb("kvm", [128, PR, 128])
        z_ready = sem("b_z_ready")
        steps = sem("b_steps")
        hdev_ready = sem("hdev_ready")
        hsq_ready = sem("hsq_ready")
        hvar_ready = sem("hvar_ready")
        hstd_ready = sem("hstd_ready")
        hn_ready = sem("hn_ready")
        k_ready = sem("b_k_ready")
        v_part = sem("b_v_part")
        v_ready = sem("b_v_ready")
        hz_added = sem("hz_added")
        zT_mm = sem("b_zT_mm")
        zT_ready = sem("b_zT_ready")
        kv_mm = sem("kv_mm")
        kvm_ready = sem("kvm_ready")
        out_mm = sem("b_out_mm")
        h_added = sem("b_h_added")
        block = ctx.enter_context(nc.Block())

        def by_head(t):
            return t[:, :, :].rearrange("p b (h d) -> p (b h) d", d=HC)

        def row(name):
            return W[name].unsqueeze(1).broadcast_to([128, GB, C])

        @block.gpsimd
        def _(pool):
            with pool.Fori(0, NG) as i:
                ln.gpsimd(pool, i)
                pool.wait_ge(z_ready, i + 1)
                nc.gpsimd.tensor_tensor(group(H, i), group(H, i), z[:, :, :], ALU.add).then_inc(hz_added, 1)
                pool.wait_ge(hvar_ready, i + 1)
                nc.gpsimd.tensor_tensor(hstd[:, :], hvar[:, :], half[:, :].broadcast_to([128, NHD]), ALU.pow)\
                    .then_inc(hstd_ready, 1)
                pool.wait_ge(hn_ready, i + 1)
                pool.wait_ge(kv_mm, i)
                nc.gpsimd.tensor_tensor(vt[:, :, :], hn[:, :, :], row("vw"), ALU.mult).then_inc(v_part, 1)
                pool.wait_ge(v_part, i + 1)
                nc.gpsimd.tensor_tensor(vt[:, :, :], vt[:, :, :], row("vb"), ALU.add).then_inc(v_ready, 1)

        @block.vector
        def _(dve):
            def front(i):
                dve.wait_ge(zT_mm, i)
                dve.wait_ge(hz_added, i)
                ln.vector(dve, i, group(H, i), z[:, :, :]).then_inc(z_ready, 1)
                dve.wait_ge(z_ready, i + 1)
                step = Steps(dve, steps, 7)
                step.begin(i)
                step(nc.vector.tensor_reduce(out=hmean[:, :], in_=by_head(z), axis=AX, op=ALU.add))
                step(nc.vector.tensor_scalar_mul(hmean[:, :], hmean[:, :], 1.0 / HC))
                nc.vector.tensor_tensor(hdev[:, :, :], by_head(z), hmean[:, :].unsqueeze(2).broadcast_to([128, NHD, HC]),
                                        ALU.subtract).then_inc(hdev_ready, 1)
                dve.wait_ge(hsq_ready, i + 1)
                step(nc.vector.tensor_reduce(out=hvar[:, :], in_=hsq[:, :, :], axis=AX, op=ALU.add))
                nc.vector.tensor_scalar_mul(hvar[:, :], hvar[:, :], 1.0 / (HC - 1)).then_inc(hvar_ready, 1)
                dve.wait_ge(hstd_ready, i + 1)
                step(nc.vector.tensor_scalar_add(hstd[:, :], hstd[:, :], EPS))
                step(nc.vector.reciprocal(hmean[:, :], hstd[:, :]))
                dve.wait_ge(v_ready, i)
                nc.vector.tensor_tensor(by_head(hn), hdev[:, :, :], hmean[:, :].unsqueeze(2).broadcast_to([128, NHD, HC]),
                                        ALU.mult).then_inc(hn_ready, 1)
                dve.wait_ge(hn_ready, i + 1)
                dve.wait_ge(kv_mm, i)
                step(nc.vector.tensor_tensor(kt[:, :, :], hn[:, :, :], row("kw"), ALU.mult))
                step(nc.vector.tensor_tensor(kt[:, :, :], kt[:, :, :], row("kb"), ALU.add))
                step.end()

            with dve.Fori(0, NG) as i:
                front(i)
                dve.wait_ge(kv_mm, i + 1)
                dve.wait_ge(out_mm, i)
                nc.vector.tensor_tensor(kvm[:, :, :], pairs(PS[:, 1, :]),
                                        W["headmask"].unsqueeze(1).broadcast_to([128, PR, 128]), ALU.mult)\
                    .then_inc(kvm_ready, 1)
                dve.wait_ge(out_mm, i + 1)
                dve.wait_ge(hz_added, i + 1)
                nc.vector.tensor_tensor(group(H, i), group(H, i), seqs(PS[:, 2, :]), ALU.add).then_inc(h_added, 1)
            dve.wait_ge(h_added, NG)

        @block.scalar
        def _(act):
            with act.Fori(0, NG) as i:
                ln.scalar(act, i)
                act.wait_ge(zT_mm, i + 1)
                act.wait_ge(out_mm, i)
                nc.scalar.activation(zT[:, :, :], pairs(PS[:, 0, :]), ACT.Copy).then_inc(zT_ready, 1)
                act.wait_ge(hdev_ready, i + 1)
                nc.scalar.activation(hsq[:, :, :], hdev[:, :, :], ACT.Square).then_inc(hsq_ready, 1)

        @block.tensor
        def _(pe):
            with pe.Fori(0, NG) as i:
                pe.wait_ge(z_ready, i + 1)
                pe.wait_ge(zT_ready, i)
                for p in range(PR):
                    mm = nc.tensor.transpose(PS[:, 0, p * 128:(p + 1) * 128], two(z, p), W["ident"])
                mm.then_inc(zT_mm, 1)
                pe.wait_ge(v_ready, i + 1)
                pe.wait_ge(steps, i * 7 + 7)
                pe.wait_ge(kvm_ready, i)
                for p in range(PR):
                    mm = nc.tensor.matmul(PS[:, 1, p * 128:(p + 1) * 128], two(kt, p), two(vt, p),
                                          start=True, stop=True)
                mm.then_inc(kv_mm, 1)
                pe.wait_ge(zT_ready, i + 1)
                pe.wait_ge(kvm_ready, i + 1)
                pe.wait_ge(h_added, i)
                for p in range(PR):
                    mm = nc.tensor.matmul(PS[:, 2, p * 128:(p + 1) * 128], zT[:, p, :], kvm[:, p, :],
                                          start=True, stop=True)
                mm.then_inc(out_mm, 1)


def split_transpose_sems(ctx, nc, tag):
    return {k: SEMS.ctx.enter_context(nc.semaphore(f"{tag}_{k}"))
            for k in ("f_ready", "hi_ready", "split_ready", "fT_mm", "fT_ready", "ft_stored", "router_mm")}


def phase_causal_attention(nc, W, PS, H, FT, WT, neg_half):
    ctx = ExitStack()
    with ctx:
        def sb(name, shape, dt=F32):
            return ctx.enter_context(nc.sbuf_tensor(name, shape, dt))

        def sem(name):
            return SEMS.ctx.enter_context(nc.semaphore(name))

        VW = HD + 1
        ln = LayerNorm(nc, ctx, "cln", neg_half)
        rms1 = RmsNorm(nc, ctx, "rms1", neg_half)
        rms2 = RmsNorm(nc, ctx, "rms2", neg_half)
        top = TopTwo(nc, ctx, "ctop", W["rev"], 1e-9, ALU.add)
        z = sb("c_z", [128, GB, C])
        hn = sb("c_hn", [128, GB, C])
        hT = sb("c_hT", [128, PR, NT])
        rope = [sb(f"rope{n}", [128, PR, NT]) for n in range(4)]
        qT = sb("c_qT", [128, PR, NT])
        kT = sb("c_kT", [128, PR, NT])
        kblk = sb("kblk", [128, PR, 2, NH, NT])
        va = sb("va", [128, GB, NKV, VW])
        nmx = sb("nmx", [128, 2, NH])
        sh = [sb(f"sh{n}", [128, NH, NT]) for n in range(2)]
        pr = [sb(f"pr{n}", [128, NH, NT]) for n in range(3)]
        pT = [sb(f"c_pT{n}", [128, NH, NT]) for n in range(2)]
        rden = sb("rden", [128, GB * NH])
        y = sb("y", [128, GB, C])
        yT = sb("yT", [128, PR, NT])
        x2 = sb("x2", [128, GB, C])
        f = sb("c_f", [128, GB, C])
        fhl = sb("c_fhl", [128, GB, 2, C])
        fTs = sb("c_fTs", [128, GB, NT])
        wrot = sb("wrot", [128, 5, 128])
        wvn = sb("wvn", [128, 64])
        router = sb("c_router", [128, NE])
        causal_b = sb("causal_b", [128, NT], BF16)
        ident_b = sb("ident_b", [128, 128], BF16)

        w_ready = sem("c_w_ready")
        blk_zero = sem("blk_zero")
        z_ready = sem("c_z_ready")
        hn_ready = sem("c_hn_ready")
        hT_mm = sem("c_hT_mm")
        hT_ready = sem("c_hT_ready")
        proj_mm = sem("proj_mm")
        rope_ready = sem("rope_ready")
        q_ready = sem("c_q_ready")
        k_ready = sem("c_k_ready")
        kblk_in = sem("kblk_in")
        va_ready = sem("va_ready")
        s_mm = sem("s_mm")
        max_ready = sem("c_max_ready")
        sub_ready = sem("sub_ready")
        exp_ready = sem("c_exp_ready")
        pT_mm = sem("c_pT_mm")
        pT_ready = sem("c_pT_ready")
        av_mm = sem("c_av_mm")
        rden_ready = sem("rden_ready")
        y_ready = sem("y_ready")
        yT_mm = sem("yT_mm")
        yT_ready = sem("yT_ready")
        wo_mm = sem("wo_mm")
        x2_ready = sem("x2_ready")
        h_added = sem("c_h_added")
        S = split_transpose_sems(ctx, nc, "c")
        w_stored = sem("c_w_stored")
        block = ctx.enter_context(nc.Block())
        wname = ["fwq", "fwqr", "fwk", "fwkr"]

        @block.sync
        def _(sp):
            sp.wait_ge(blk_zero, 2)
            with sp.Fori(0, NG) as i:
                sp.wait_ge(k_ready, i + 1)
                for b in range(2):
                    for h in range(NH):
                        r = slice(64 * b + HD * h, 64 * b + HD * h + HD)
                        sp.dma_start(kblk[r, :, b, h, :], kT[r, :, :]).then_inc(kblk_in, 16)
            sp.wait_ge(kblk_in, NG * 128)

        @block.gpsimd
        def _(pool):
            nc.gpsimd.memset(kblk[:, :, :, :, :], 0.0).then_inc(blk_zero, 1)
            nc.gpsimd.memset(va[:, :, :, HD:VW], 1.0).then_inc(blk_zero, 1)
            with pool.Fori(0, NG) as i:
                ln.gpsimd(pool, i)
                rms1.gpsimd(pool, i)
                pool.wait_ge(rope_ready, i * 4 + 2)
                pool.wait_ge(s_mm, i * GB)
                nc.gpsimd.tensor_tensor(kT[:, :, :], rope[0][:, :, :], rope[1][:, :, :], ALU.add).then_inc(k_ready, 1)
                pool.wait_ge(rope_ready, i * 4 + 4)
                nc.gpsimd.tensor_tensor(qT[:, :, :], rope[2][:, :, :], rope[3][:, :, :], ALU.add).then_inc(q_ready, 1)
                pool.wait_ge(x2_ready, i + 1)
                nc.gpsimd.tensor_tensor(group(H, i), group(H, i), x2[:, :, :], ALU.add).then_inc(h_added, 1)
                rms2.gpsimd(pool, i)

        @block.tensor
        def _(pe):
            def scores(i, u):
                p, b = u // 2, u % 2
                if u < 2:
                    pe.wait_ge(sub_ready, i * GB)
                else:
                    pe.wait_ge(sub_ready, i * GB + u - 1)
                nc.tensor.matmul(PS[:, 6 + u % 2, :], ident_b[:, :], causal_b[:, :].unsqueeze(1).broadcast_to([128, NH, NT]),
                                 start=True, stop=False)
                nc.tensor.matmul(PS[:, 6 + u % 2, :], qT[:, p, :], kblk[:, p, b, :, :],
                                 start=False, stop=True).then_inc(s_mm, 1)

            def turn(i, u):
                pe.wait_ge(exp_ready, i * GB + u + 1)
                if u >= 2:
                    pe.wait_ge(pT_ready, i * GB + u - 1)
                for h in range(NH):
                    mm = nc.tensor.transpose(PS[:, 1 + u % 2, h * NT:(h + 1) * NT], pr[u % 3][:, h, :], W["ident"])
                mm.then_inc(pT_mm, 1)

            def values(i, u):
                pe.wait_ge(pT_ready, i * GB + u + 1)
                if u == 0:
                    pe.wait_ge(va_ready, i + 1)
                for h in range(NH):
                    at = ((u % 4) * NH + h) * VW
                    mm = nc.tensor.matmul(PS[:, 3 + u // 4, at:at + VW], pT[u % 2][:, h, :],
                                          va[:, u, h // (NH // NKV), :], start=True, stop=True)
                mm.then_inc(av_mm, 1)

            pe.wait_ge(w_ready, 1)
            with pe.Fori(0, NG) as i:
                pe.wait_ge(hn_ready, i + 1)
                pe.wait_ge(x2_ready, i)
                for p in range(PR):
                    mm = nc.tensor.transpose(PS[:, 0, p * 128:(p + 1) * 128], two(hn, p), W["ident"])
                mm.then_inc(hT_mm, 1)
                pe.wait_ge(hT_ready, i + 1)
                pe.wait_ge(y_ready, i * 2)
                pe.wait_ge(w_stored, i)
                for n in (2, 3, 0, 1):
                    nc.tensor.matmul(PS[:, 1 + n, :], wrot[:, n, :], hT[:, :, :], start=True, stop=True)\
                        .then_inc(proj_mm, 1)
                for p in range(PR):
                    mm = nc.tensor.matmul(PS[:, 5, p * 64:(p + 1) * 64], hT[:, p, :], wvn[:, :], start=True, stop=True)
                mm.then_inc(proj_mm, 1)
                pe.wait_ge(q_ready, i + 1)
                pe.wait_ge(kblk_in, i * 128 + 128)
                for t in range(GB + 3):
                    if t < GB:
                        scores(i, t)
                    if 2 <= t < GB + 2:
                        turn(i, t - 2)
                    if 3 <= t:
                        values(i, t - 3)
                for hf in range(2):
                    pe.wait_ge(y_ready, i * 2 + hf + 1)
                    for p in (2 * hf, 2 * hf + 1):
                        mm = nc.tensor.transpose(PS[:, 5, p * 128:(p + 1) * 128], two(y, p), W["ident"])
                mm.then_inc(yT_mm, 1)
                pe.wait_ge(yT_ready, i + 1)
                for p in range(PR):
                    mm = nc.tensor.matmul(PS[:, 0, p * 128:(p + 1) * 128], yT[:, p, :], W["fwo"], start=True, stop=True)
                mm.then_inc(wo_mm, 1)
                split_tensor(nc, pe, i, S, PS, (6, 7), 5, fhl, fTs, router, W["ident"])

        @block.scalar
        def _(act):
            with act.Fori(0, NG) as i:
                ln.scalar(act, i)
                act.wait_ge(z_ready, i + 1)
                rms1.scalar(act, i, z[:, :, :])
                act.wait_ge(hT_mm, i + 1)
                nc.scalar.activation(hT[:, :, :], pairs(PS[:, 0, :]), ACT.Copy).then_inc(hT_ready, 1)
                act.wait_ge(proj_mm, i * 5 + 5)
                act.wait_ge(av_mm, i * GB)
                nc.scalar.activation(va[:, :, :, 0:HD],
                                     PS[:, 5, 0:256].rearrange("p (b k d) -> p b k d", b=GB, k=NKV), ACT.Copy)\
                    .then_inc(va_ready, 1)
                for t in range(GB + 2):
                    if t < GB:
                        act.wait_ge(sub_ready, i * GB + t + 1)
                        if t >= 3:
                            act.wait_ge(pT_mm, i * GB + t - 2)
                        nc.scalar.activation(pr[t % 3][:, :, :], sh[t % 2][:, :, :], ACT.Exp).then_inc(exp_ready, 1)
                    if t >= 2:
                        u = t - 2
                        act.wait_ge(pT_mm, i * GB + u + 1)
                        if u >= 2:
                            act.wait_ge(av_mm, i * GB + u - 1)
                        nc.scalar.activation(pT[u % 2][:, :, :], PS[:, 1 + u % 2, :].rearrange("p (h s) -> p h s", h=NH),
                                             ACT.Copy).then_inc(pT_ready, 1)
                act.wait_ge(yT_mm, i + 1)
                nc.scalar.activation(yT[:, :, :], pairs(PS[:, 5, :]), ACT.Copy).then_inc(yT_ready, 1)
                act.wait_ge(x2_ready, i + 1)
                rms2.scalar(act, i, x2[:, :, :])
                split_scalar(nc, act, i, S, PS, (6, 7), fTs)
                top.scalar(act, i)

        @block.vector
        def _(dve):
            nc.vector.tensor_copy(causal_b[:, :], W["causal"])
            nc.vector.tensor_copy(ident_b[:, :], W["ident"])
            for n in range(4):
                nc.vector.tensor_scalar(wrot[:, n, :], W[wname[n]], W["ln1"], None, ALU.mult)
            nc.vector.tensor_scalar(wvn[:, :], W["fwv"], W["ln1"], None, ALU.mult)
            nc.vector.tensor_scalar(router[:, :], W["frouter"], W["ln2"], None, ALU.mult).then_inc(w_ready, 1)
            with dve.Fori(0, NG) as i:
                dve.wait_ge(h_added, i)
                ln.vector(dve, i, group(H, i), z[:, :, :]).then_inc(z_ready, 1)
                dve.wait_ge(z_ready, i + 1)
                dve.wait_ge(hT_mm, i)
                rms1.vector(dve, i, z[:, :, :], hn[:, :, :]).then_inc(hn_ready, 1)
                dve.wait_ge(k_ready, i)
                dve.wait_ge(q_ready, i)
                for n, (bank, table) in enumerate(((3, "cosk"), (4, "sink"), (1, "cosq"), (2, "sinq"))):
                    dve.wait_ge(proj_mm, i * 5 + n + 1)
                    nc.vector.tensor_tensor(rope[n][:, :, :], pairs(PS[:, bank, :]),
                                            W[table].unsqueeze(1).broadcast_to([128, PR, NT]), ALU.mult)\
                        .then_inc(rope_ready, 1)
                for u in range(GB):
                    bank = PS[:, 6 + u % 2, :].rearrange("p (h s) -> p h s", h=NH)
                    dve.wait_ge(s_mm, i * GB + u + 1)
                    nc.vector.tensor_reduce(out=nmx[:, u % 2, :], in_=bank, axis=AX, op=ALU.max).then_inc(max_ready, 1)
                    dve.wait_ge(max_ready, i * GB + u + 1)
                    if u >= 2:
                        dve.wait_ge(exp_ready, i * GB + u - 1)
                    nc.vector.tensor_tensor(sh[u % 2][:, :, :], bank, nmx[:, u % 2, :].unsqueeze(2).broadcast_to([128, NH, NT]),
                                            ALU.subtract).then_inc(sub_ready, 1)
                for hf in range(2):
                    dve.wait_ge(av_mm, i * GB + 4 * hf + 4)
                    o = PS[:, 3 + hf, 0:4 * NH * VW].rearrange("p (a d) -> p a d", d=VW)
                    rd = rden[:, hf * 4 * NH:(hf + 1) * 4 * NH]
                    nc.vector.reciprocal(rd.unsqueeze(2), o[:, :, HD:VW]).then_inc(rden_ready, 1)
                    dve.wait_ge(rden_ready, i * 2 + hf + 1)
                    nc.vector.tensor_tensor(y[:, 4 * hf:4 * hf + 4, :].rearrange("p b (h d) -> p (b h) d", h=NH),
                                            o[:, :, 0:HD], rd.unsqueeze(2).broadcast_to([128, 4 * NH, HD]), ALU.mult)\
                        .then_inc(y_ready, 1)
                dve.wait_ge(wo_mm, i + 1)
                nc.vector.tensor_tensor(x2[:, :, :], z[:, :, :], seqs(PS[:, 0, :]), ALU.add).then_inc(x2_ready, 1)
                rms2.vector(dve, i, x2[:, :, :], f[:, :, :]).then_inc(S["f_ready"], 1)
                split_vector(nc, dve, i, S, f, fhl, fTs, FT)
                dve.wait_ge(S["router_mm"], i + 1)
                top.vector(dve, i, PS[:, 5, 0:GB * NE].rearrange("p (b e) -> p b e", b=GB), group(WT, i))\
                    .then_inc(w_stored, 1)
            dve.wait_ge(w_stored, NG)


def split_vector(nc, dve, i, S, f, fhl, fTs, FT):
    dve.wait_ge(S["f_ready"], i + 1)
    dve.wait_ge(S["fT_mm"], i * 2)
    nc.vector.tensor_copy(fhl[:, :, 0, :].bitcast(F32R), f[:, :, :]).then_inc(S["hi_ready"], 1)
    dve.wait_ge(S["hi_ready"], i + 1)
    nc.vector.tensor_tensor(fhl[:, :, 1, :], f[:, :, :], fhl[:, :, 0, :], ALU.subtract).then_inc(S["split_ready"], 1)
    dve.wait_ge(S["fT_ready"], i * 2 + 2)
    nc.vector.tensor_copy(FT[:, bass.ds(i * GB, GB), :].bitcast(F32R), fTs[:, :, :]).then_inc(S["ft_stored"], 1)


def split_tensor(nc, pe, i, S, PS, banks, logit_bank, fhl, fTs, router, ident):
    pe.wait_ge(S["split_ready"], i + 1)
    for n in range(2):
        for s in range(4):
            mm = nc.tensor.transpose(PS[:, banks[n], s * 128:(s + 1) * 128],
                                     fhl[:, 4 * n + s, :, :].rearrange("p a b -> p (a b)"), ident)
        mm.then_inc(S["fT_mm"], 1)
    pe.wait_ge(S["fT_ready"], i * 2 + 2)
    for s in range(GB):
        mm = nc.tensor.matmul(PS[:, logit_bank, s * NE:(s + 1) * NE], fTs[:, s, :], router[:, :], start=True, stop=True)
    mm.then_inc(S["router_mm"], 1)


def split_scalar(nc, act, i, S, PS, banks, fTs):
    act.wait_ge(S["router_mm"], i)
    act.wait_ge(S["ft_stored"], i)
    for n in range(2):
        act.wait_ge(S["fT_mm"], i * 2 + n + 1)
        nc.scalar.activation(fTs[:, 4 * n:4 * n + 4, :], pairs(PS[:, banks[n], :]), ACT.Copy).then_inc(S["fT_ready"], 1)


TS = 4
NTILE = B // TS


def combine(nc, dve, i, PS, down_mm, comb_mult, comb_red, h_added, ws, ws_ready, tmp, ys):
    dve.wait_ge(ws_ready, i + 1)
    for q in range(TS):
        dve.wait_ge(down_mm, i * TS + q + 1)
        if q >= 2:
            dve.wait_ge(comb_red, i * TS + q - 1)
        else:
            dve.wait_ge(comb_red, i * TS)
        nc.vector.tensor_tensor(tmp[q % 2][:, :, :], PS[:, 6 + q % 2, :].rearrange("p (e c) -> p e c", e=NE),
                                ws[:, q, :].unsqueeze(2).broadcast_to([128, NE, C]), ALU.mult).then_inc(comb_mult, 1)
        dve.wait_ge(comb_mult, i * TS + q + 1)
        if q == 0:
            dve.wait_ge(h_added, i)
        nc.vector.tensor_reduce(out=ys[:, q, :], in_=tmp[q % 2][:, :, :].rearrange("p e c -> p c e"),
                                axis=AX, op=ALU.add).then_inc(comb_red, 1)


def phase_swiglu_experts(nc, W, PS, H, FT, WT):
    ctx = ExitStack()
    with ctx:
        def sb(name, shape, dt=F32):
            return ctx.enter_context(nc.sbuf_tensor(name, shape, dt))

        def sem(name):
            return SEMS.ctx.enter_context(nc.semaphore(name))

        wh = sb("d_wh", [128, NJ, 2, 128])
        wl = sb("d_wl", [128, NJ, 2, 128])
        sa = [sb(f"sa{n}", [128, 512]) for n in range(3)]
        hh = sb("hh", [128, NJ, 512])
        ws = sb("d_ws", [128, TS, NE])
        tmp = [sb(f"d_tmp{n}", [128, NE, C]) for n in range(2)]
        ys = sb("d_ys", [128, TS, C])
        w_steps = sem("d_w_steps")
        up_mm = sem("up_mm")
        silu_ready = sem("silu_ready")
        hh_ready = sem("hh_ready")
        down_mm = sem("down_mm")
        ws_ready = sem("d_ws_ready")
        comb_mult = sem("d_comb_mult")
        comb_red = sem("d_comb_red")
        h_added = sem("d_h_added")
        block = ctx.enter_context(nc.Block())
        w13 = W["w13"].rearrange("p (j n m) -> p j n m", j=NJ, n=2)
        w2 = W["w2"].rearrange("p (e c) -> p e c", e=NE)
        w2r = W["w2r"].rearrange("p (t c) -> p t c", t=NJ - NE)
        ft = FT[:, :, :].rearrange("p b t -> p (b t)")

        @block.gpsimd
        def _(pool):
            with pool.Fori(0, NTILE) as i:
                pool.wait_ge(comb_red, i * TS)
                nc.gpsimd.tensor_copy(ws[:, :, :], WT[:, bass.ds(i * TS, TS), :]).then_inc(ws_ready, 1)
                pool.wait_ge(comb_red, i * TS + TS)
                h = H[:, bass.ds(i * TS, TS), :]
                nc.gpsimd.tensor_tensor(h, h, ys[:, :, :], ALU.add).then_inc(h_added, 1)
            pool.wait_ge(h_added, NTILE)

        @block.tensor
        def _(pe):
            pe.wait_ge(w_steps, 3)
            with pe.Fori(0, NTILE) as i:
                for j in range(NJ):
                    s = j % 3
                    if j >= 3:
                        pe.wait_ge(hh_ready, i * NJ + j - 2)
                    else:
                        pe.wait_ge(hh_ready, i * NJ)
                    for n in range(2):
                        for k, w in enumerate((wh, wl)):
                            mm = nc.tensor.matmul(PS[:, 2 * s + n, :], w[:, j, n, :].bitcast(F32R),
                                                  ft[:, bass.ds(i * 512, 512)].bitcast(F32R), start=(k == 0), stop=(k == 1))
                        mm.then_inc(up_mm, 1)
                pe.wait_ge(hh_ready, i * NJ + NJ)
                for q in range(TS):
                    if q >= 2:
                        pe.wait_ge(comb_mult, i * TS + q - 1)
                    else:
                        pe.wait_ge(comb_mult, i * TS)
                    o = PS[:, 6 + q % 2, :]
                    for t in range(NJ - NE):
                        es = range(t * RT, min((t + 1) * RT, NE))
                        nc.tensor.matmul(o[:, es[0] * C:(es[-1] + 1) * C], hh[:, NE + t, q * NT:(q + 1) * NT],
                                         w2r[:, t, 0:len(es) * C], start=True, stop=False)
                        for e in es:
                            mm = nc.tensor.matmul(o[:, e * C:(e + 1) * C], hh[:, e, q * NT:(q + 1) * NT], w2[:, e, :],
                                                  start=False, stop=(e == es[-1]))
                    mm.then_inc(down_mm, 1)

        @block.scalar
        def _(act):
            with act.Fori(0, NTILE) as i:
                for j in range(NJ):
                    act.wait_ge(up_mm, i * 2 * NJ + 2 * j + 1)
                    if j >= 3:
                        act.wait_ge(hh_ready, i * NJ + j - 2)
                    else:
                        act.wait_ge(hh_ready, i * NJ)
                    nc.scalar.activation(sa[j % 3][:, :], PS[:, 2 * (j % 3), :], ACT.Silu).then_inc(silu_ready, 1)

        @block.vector
        def _(dve):
            nc.vector.tensor_scalar(w13, w13, W["ln2"], None, ALU.mult).then_inc(w_steps, 1)
            dve.wait_ge(w_steps, 1)
            nc.vector.tensor_copy(wh[:, :, :, :].bitcast(F32R), w13).then_inc(w_steps, 1)
            dve.wait_ge(w_steps, 2)
            nc.vector.tensor_tensor(wl[:, :, :, :].bitcast(F32R), w13, wh[:, :, :, :], ALU.subtract).then_inc(w_steps, 1)
            with dve.Fori(0, NTILE) as i:
                dve.wait_ge(down_mm, i * TS)
                for j in range(NJ):
                    dve.wait_ge(silu_ready, i * NJ + j + 1)
                    dve.wait_ge(up_mm, i * 2 * NJ + 2 * j + 2)
                    nc.vector.tensor_tensor(hh[:, j, :], PS[:, 2 * (j % 3) + 1, :], sa[j % 3][:, :], ALU.mult)\
                        .then_inc(hh_ready, 1)
                combine(nc, dve, i, PS, down_mm, comb_mult, comb_red, h_added, ws, ws_ready, tmp, ys)


def phase_relu_attention(nc, W, PS, H, FT, WT, neg_half):
    ctx = ExitStack()
    with ctx:
        def sb(name, shape, dt=F32):
            return ctx.enter_context(nc.sbuf_tensor(name, shape, dt))

        def sem(name):
            return SEMS.ctx.enter_context(nc.semaphore(name))

        ln3 = LayerNorm(nc, ctx, "ln3", neg_half)
        ln4 = LayerNorm(nc, ctx, "ln4", neg_half)
        top = TopTwo(nc, ctx, "etop", W["rev"], 1e-12, ALU.max)
        wqk = sb("wqk", [128, 2, 128])
        wvo = sb("wvo", [128, 128])
        z = sb("e_z", [128, GB, C])
        zT = sb("e_zT", [128, PR, NT])
        uT = sb("uT", [128, PR, 2, NT])
        vs = sb("e_vs", [128, GB, C])
        pm = sb("pm", [128, GB, NT])
        h2 = sb("e_h2", [128, GB, C])
        z4 = sb("z4", [128, GB, C])
        fhl = sb("e_fhl", [128, GB, 2, C])
        fTs = sb("e_fTs", [128, GB, NT])
        wsp = sb("e_ws", [128, 2 * GB, NE])
        ws = wsp[:, 0:GB, :]
        wTs = sb("wTs", [128, NT])
        res = sb("res", [128, GB, C])
        w_mm = sem("e_w_mm")
        w_ready = sem("e_w_ready")
        z_ready = sem("e_z_ready")
        zT_mm = sem("e_zT_mm")
        zT_ready = sem("e_zT_ready")
        proj_mm = sem("e_proj_mm")
        proj_ready = sem("e_proj_ready")
        s_mm = sem("e_s_mm")
        pm_ready = sem("pm_ready")
        av_mm = sem("e_av_mm")
        h2_ready = sem("e_h2_ready")
        S = split_transpose_sems(ctx, nc, "e")
        ws_ready = sem("e_ws_ready")
        wt_stored = sem("wt_stored")
        wT_mm = sem("wT_mm")
        wT_ready = sem("wT_ready")
        b2_mm = sem("b2_mm")
        res_ready = sem("res_ready")
        h_stored = sem("e_h_stored")
        block = ctx.enter_context(nc.Block())

        @block.gpsimd
        def _(pool):
            with pool.Fori(0, NG) as i:
                ln3.gpsimd(pool, i)
                ln4.gpsimd(pool, i)
                pool.wait_ge(ws_ready, i + 1)
                nc.gpsimd.tensor_copy(group(WT, i), ws).then_inc(wt_stored, 1)
                pool.wait_ge(res_ready, i + 1)
                nc.gpsimd.tensor_tensor(group(H, i), res[:, :, :], h2[:, :, :], ALU.add).then_inc(h_stored, 1)
            pool.wait_ge(h_stored, NG)
            pool.wait_ge(wt_stored, NG)

        @block.tensor
        def _(pe):
            nc.tensor.matmul(PS[:, 0, 0:128], W["awq"], W["awk"], start=True, stop=True).then_inc(w_mm, 1)
            nc.tensor.matmul(PS[:, 1, 0:128], W["awv"], W["awo"], start=True, stop=True).then_inc(w_mm, 1)
            pe.wait_ge(w_ready, 3)
            with pe.Fori(0, NG) as i:
                pe.wait_ge(z_ready, i + 1)
                pe.wait_ge(S["ft_stored"], i)
                pe.wait_ge(res_ready, i)
                for p in range(PR):
                    mm = nc.tensor.transpose(PS[:, 0, p * 128:(p + 1) * 128], two(z, p), W["ident"])
                mm.then_inc(zT_mm, 1)
                pe.wait_ge(zT_ready, i + 1)
                for b in range(2):
                    nc.tensor.matmul(PS[:, 1 + b, :], wqk[:, b, :], zT[:, :, :], start=True, stop=True)\
                        .then_inc(proj_mm, 1)
                for p in range(PR):
                    mm = nc.tensor.matmul(PS[:, 3, p * 128:(p + 1) * 128], zT[:, p, :], wvo[:, :], start=True, stop=True)
                mm.then_inc(proj_mm, 1)
                pe.wait_ge(proj_ready, i * 3 + 3)
                for p in range(PR):
                    mm = nc.tensor.matmul(PS[:, 4 + p // 2, (p % 2) * 256:(p % 2) * 256 + 256], zT[:, p, :], uT[:, p, :, :],
                                          start=True, stop=True)
                    if p % 2:
                        mm.then_inc(s_mm, 1)
                for s in range(GB):
                    if s % 4 == 0:
                        pe.wait_ge(pm_ready, i * 2 + s // 4 + 1)
                    mm = nc.tensor.matmul(PS[:, 0, s * C:(s + 1) * C], pm[:, s, :], vs[:, s, :], start=True, stop=True)
                mm.then_inc(av_mm, 1)
                split_tensor(nc, pe, i, S, PS, (6, 7), 1, fhl, fTs, W["grouter"], W["ident"])
                pe.wait_ge(ws_ready, i + 1)
                nc.tensor.transpose(PS[:, 2, 0:128], wsp[:, :, :].rearrange("p b e -> p (b e)"), W["ident"])\
                    .then_inc(wT_mm, 1)
                pe.wait_ge(wT_ready, i + 1)
                nc.tensor.matmul(PS[:, 3, :], wTs[:, :], W["gb2"], start=True, stop=True).then_inc(b2_mm, 1)

        @block.scalar
        def _(act):
            with act.Fori(0, NG) as i:
                ln3.scalar(act, i)
                act.wait_ge(zT_mm, i + 1)
                nc.scalar.activation(zT[:, :, :], pairs(PS[:, 0, :]), ACT.Copy).then_inc(zT_ready, 1)
                for b in range(2):
                    act.wait_ge(proj_mm, i * 3 + b + 1)
                    nc.scalar.activation(uT[:, :, b, :], pairs(PS[:, 1 + b, :]), ACT.Copy).then_inc(proj_ready, 1)
                act.wait_ge(proj_mm, i * 3 + 3)
                nc.scalar.activation(vs[:, :, :], seqs(PS[:, 3, :]), ACT.Copy).then_inc(proj_ready, 1)
                ln4.scalar(act, i)
                split_scalar(nc, act, i, S, PS, (6, 7), fTs)
                top.scalar(act, i)
                act.wait_ge(wT_mm, i + 1)
                nc.scalar.activation(wTs[:, :], PS[:, 2, 0:128], ACT.Copy).then_inc(wT_ready, 1)

        @block.vector
        def _(dve):
            dve.wait_ge(w_mm, 2)
            nc.vector.memset(wsp[:, GB:2 * GB, :], 0.0)
            nc.vector.memset(wqk[:, :, :], 0.0).then_inc(w_ready, 1)
            dve.wait_ge(w_ready, 1)
            nc.vector.tensor_copy(wqk[0:64, 0, 0:64], PS[0:64, 0, 0:64])
            nc.vector.tensor_copy(wqk[64:128, 1, 64:128], PS[64:128, 0, 64:128]).then_inc(w_ready, 1)
            nc.vector.tensor_copy(wvo[:, :], PS[:, 1, 0:128]).then_inc(w_ready, 1)
            with dve.Fori(0, NG) as i:
                dve.wait_ge(h_stored, i)
                ln3.vector(dve, i, group(H, i), z[:, :, :]).then_inc(z_ready, 1)
                for n in range(2):
                    dve.wait_ge(s_mm, i * 2 + n + 1)
                    nc.vector.scalar_tensor_tensor(out=pm[:, 4 * n:4 * n + 4, :], in0=pairs(PS[:, 4 + n, :]), scalar=0.0,
                                                   in1=W["relumask"].unsqueeze(1).broadcast_to([128, 4, NT]),
                                                   op0=ALU.max, op1=ALU.mult).then_inc(pm_ready, 1)
                dve.wait_ge(av_mm, i + 1)
                nc.vector.tensor_tensor(h2[:, :, :], group(H, i), seqs(PS[:, 0, :]), ALU.add).then_inc(h2_ready, 1)
                dve.wait_ge(h2_ready, i + 1)
                ln4.vector(dve, i, h2[:, :, :], z4[:, :, :]).then_inc(S["f_ready"], 1)
                split_vector(nc, dve, i, S, z4, fhl, fTs, FT)
                dve.wait_ge(S["router_mm"], i + 1)
                dve.wait_ge(wt_stored, i)
                top.vector(dve, i, PS[:, 1, 0:GB * NE].rearrange("p (b e) -> p b e", b=GB), ws)\
                    .then_inc(ws_ready, 1)
                dve.wait_ge(b2_mm, i + 1)
                nc.vector.tensor_tensor(res[:, :, :], z4[:, :, :], seqs(PS[:, 3, :]), ALU.add).then_inc(res_ready, 1)


def phase_gelu_experts(nc, W, PS, H, FT, WT, out):
    ctx = ExitStack()
    with ctx:
        def sb(name, shape, dt=F32):
            return ctx.enter_context(nc.sbuf_tensor(name, shape, dt))

        def sem(name):
            return SEMS.ctx.enter_context(nc.semaphore(name))

        NK = NE // 2
        wh = sb("f_wh", [128, NK, 128])
        wl = sb("f_wl", [128, NK, 128])
        gg = sb("gg", [128, NK, 512])
        ws = sb("f_ws", [128, TS, NE])
        tmp = [sb(f"f_tmp{n}", [128, NE, C]) for n in range(2)]
        ys = sb("f_ys", [128, TS, C])
        fin = sb("fin", [128, TS, C])
        w_steps = sem("f_w_steps")
        up_mm = sem("f_up_mm")
        gg_ready = sem("gg_ready")
        down_mm = sem("f_down_mm")
        ws_ready = sem("f_ws_ready")
        comb_mult = sem("f_comb_mult")
        comb_red = sem("f_comb_red")
        fin_ready = sem("fin_ready")
        stored = sem("out_stored")
        block = ctx.enter_context(nc.Block())
        w1 = W["gw1"].rearrange("p (j m) -> p j m", j=NK)
        w2 = W["gw2"].rearrange("p (j m) -> p j m", j=NK)
        ft = FT[:, :, :].rearrange("p b t -> p (b t)")
        ov = out.rearrange("b n t -> n b t")

        @block.sync
        def _(sp):
            with sp.Fori(0, NTILE) as i:
                sp.wait_ge(fin_ready, i + 1)
                sp.dma_start(ov[:, bass.ds(i * TS, TS), :], fin[:, :, :]).then_inc(stored, 16)
            sp.wait_ge(stored, NTILE * 16)

        @block.gpsimd
        def _(pool):
            with pool.Fori(0, NTILE) as i:
                pool.wait_ge(comb_red, i * TS)
                nc.gpsimd.tensor_copy(ws[:, :, :], WT[:, bass.ds(i * TS, TS), :]).then_inc(ws_ready, 1)
                pool.wait_ge(comb_red, i * TS + TS)
                pool.wait_ge(stored, i * 16)
                nc.gpsimd.tensor_tensor(fin[:, :, :], H[:, bass.ds(i * TS, TS), :], ys[:, :, :], ALU.add)\
                    .then_inc(fin_ready, 1)

        @block.tensor
        def _(pe):
            pe.wait_ge(w_steps, 2)
            with pe.Fori(0, NTILE) as i:
                pe.wait_ge(gg_ready, i * NK)
                for j in range(NK):
                    for k, w in enumerate((wh, wl)):
                        mm = nc.tensor.matmul(PS[:, j, :], w[:, j, :].bitcast(F32R),
                                              ft[:, bass.ds(i * 512, 512)].bitcast(F32R), start=(k == 0), stop=(k == 1))
                    mm.then_inc(up_mm, 1)
                pe.wait_ge(gg_ready, i * NK + NK)
                for q in range(TS):
                    if q >= 2:
                        pe.wait_ge(comb_mult, i * TS + q - 1)
                    else:
                        pe.wait_ge(comb_mult, i * TS)
                    for j in range(NK):
                        mm = nc.tensor.matmul(PS[:, 6 + q % 2, j * 128:(j + 1) * 128], gg[:, j, q * NT:(q + 1) * NT],
                                              w2[:, j, :], start=True, stop=True)
                    mm.then_inc(down_mm, 1)

        @block.scalar
        def _(act):
            with act.Fori(0, NTILE) as i:
                act.wait_ge(down_mm, i * TS)
                for j in range(NK):
                    act.wait_ge(up_mm, i * NK + j + 1)
                    nc.scalar.activation(gg[:, j, :], PS[:, j, :], ACT.Gelu, bias=W["gb1"][:, j:j + 1])\
                        .then_inc(gg_ready, 1)

        @block.vector
        def _(dve):
            nc.vector.tensor_copy(wh[:, :, :].bitcast(F32R), w1).then_inc(w_steps, 1)
            dve.wait_ge(w_steps, 1)
            nc.vector.tensor_tensor(wl[:, :, :].bitcast(F32R), w1, wh[:, :, :], ALU.subtract).then_inc(w_steps, 1)
            with dve.Fori(0, NTILE) as i:
                combine(nc, dve, i, PS, down_mm, comb_mult, comb_red, fin_ready, ws, ws_ready, tmp, ys)


def phase_dump(nc, H, out):
    ctx = ExitStack()
    with ctx:
        done = ctx.enter_context(nc.semaphore("dumped"))
        block = ctx.enter_context(nc.Block())

        @block.sync
        def _(sp):
            sp.dma_start(out.rearrange("b n t -> n b t"), H[:, :, :]).then_inc(done, 16)
            sp.wait_ge(done, 16)


def constants():
    r = np.arange(128)
    inv_freq = 1.0 / 10000.0 ** (np.arange(0, HD, 2, dtype=np.float32) / HD)
    freqs = np.outer(np.arange(NT, dtype=np.float32), inv_freq)
    emb = np.concatenate([freqs, freqs], axis=-1)
    d = r % HD
    cos, sin = np.cos(emb).T[d].astype(np.float32), np.sin(emb).T[d].astype(np.float32)
    sin = np.where((d < HD // 2)[:, None], -sin, sin)
    head = (r % 64) // HD
    c = {
        "ident": np.eye(128),
        "headmask": (r[:, None] // HC == r[None, :] // HC) / NT,
        "causal": np.where(r[None, :] <= r[:, None], 0.0, -1e30),
        "cosq": cos / np.sqrt(HD), "sinq": sin / np.sqrt(HD), "cosk": cos, "sink": sin,
        "hsel": head[:, None] == np.arange(NH)[None, :],
        "rev": np.broadcast_to(np.arange(NE, 0, -1), (128, NE)),
        "relumask": (r[:, None] <= r[None, :]) / np.maximum(r[None, :], 1),
    }
    return {k: np.asarray(v, np.float32) for k, v in c.items()}


def lay_out(a):
    a = {k: np.asarray(v) for k, v in a.items()}

    def zeros(*s):
        return np.zeros(s, np.float32)

    def diag2(m):
        k, n = m.shape
        o = zeros(2 * k, 2 * n)
        o[:k, :n] = m
        o[k:, n:] = m
        return o

    def col(v, n):
        return np.tile(v, n)[:, None]

    def full(m):
        o = zeros(128, m.shape[1])
        o[:m.shape[0]] = m
        return o

    p = "L0_tok_"
    L = constants()
    w1, w2 = a[p + "w1"], a[p + "w2"]
    w1t = zeros(2, 64, GB, C1)
    w2t = zeros(PR, 2, C1, 3, 2, C2)
    for b in range(GB):
        for tap in range(3):
            at = tap * 16 + b * 2
            w1t[:, at:at + 2, b, :] = w1[:, :, tap].T
    for b in range(2):
        w2t[:, b, :, :, b, :] = w2.transpose(1, 2, 0)
    L["w1t"] = w1t.reshape(128, 128)
    L["w2t"] = w2t.reshape(128, 3 * 128)
    for n, reps in (("1", GB), ("2", 2)):
        for k in "gv":
            L[f"{k}{n}row"] = np.broadcast_to(np.tile(a[p + k + n], reps)[None, :], (128, 128))
    wq, wk = zeros(128, 64), zeros(128, 64)
    bq, bk = zeros(128, 1), zeros(128, 1)
    for b in range(2):
        wq[64 * b:64 * b + 64, 32 * b:32 * b + CQ] = a[p + "wq"].T
        wk[64 * b:64 * b + 64, 32 * b:32 * b + CQ] = a[p + "wk"].T
        bq[32 * b:32 * b + CQ, 0] = a[p + "bq"]
        bk[32 * b:32 * b + CQ, 0] = a[p + "bk"]
    L.update(wq=wq, wk=wk, bq=bq, bk=bk, wv=diag2(a[p + "wv"].T), bv=col(a[p + "bv"], 2))
    w3 = a[p + "w3"].transpose(1, 2, 0).reshape(C2, 4 * 128)
    L["w3t"] = np.concatenate([w3, w3], axis=0)
    L["gamma"] = np.broadcast_to(a[p + "gamma"].reshape(1, 1), (128, 1))
    for k in ("b", "g", "be", "m", "v"):
        L["c" + k] = np.concatenate([col(a[f"{p}{k}1"], GB), col(a[f"{p}{k}2"], 2), col(a[f"{p}{k}3"], 1)], axis=1)
    p = "L0_attn_"
    for k, n in (("kw", "kln_weight"), ("kb", "kln_bias"), ("vw", "vln_weight"), ("vb", "vln_bias")):
        L[k] = np.broadcast_to(a[p + n].reshape(1, C), (128, C))
    p = "L0_ffn_"
    L["ln1"], L["ln2"] = col(a[p + "ln1_w"], 2), col(a[p + "ln2_w"], 2)
    q = a[p + "wq"].reshape(NH, HD, C)
    k = np.repeat(a[p + "wk"].reshape(NKV, HD, C), NH // NKV, axis=0)
    for n, m in (("q", q), ("k", k)):
        L["fw" + n] = diag2(m.reshape(NH * HD, C).T)
        L["fw" + n + "r"] = diag2(np.concatenate([m[:, HD // 2:], m[:, :HD // 2]], axis=1).reshape(NH * HD, C).T)
    L["fwv"] = diag2(a[p + "wv"].T)
    L["fwo"] = diag2(a[p + "wo"].T)
    L["frouter"] = np.concatenate([a[p + "router_w"].T] * 2, axis=0)
    w13, w2m, w2r = zeros(2, C, NJ, 2, 128), zeros(128, NE, C), zeros(128, NJ - NE, RT, C)
    for e in range(NE):
        t, s = NE + e // RT, e % RT
        for n, w in enumerate((a[p + "w1"][e], a[p + "w3"][e])):
            w13[:, :, e, n, :] = w[:128].T
            w13[:, :, t, n, s * REM:(s + 1) * REM] = w[128:].T
        w = a[p + "w2"][e].T
        w2m[:, e] = w[:128]
        w2r[s * REM:(s + 1) * REM, e // RT, s] = w[128:]
    L.update(w13=w13.reshape(128, -1), w2=w2m.reshape(128, -1), w2r=w2r.reshape(128, -1))
    p = "L1_attn_"
    L.update(awq=diag2(a[p + "Wq"]), awk=diag2(a[p + "Wk"]), awv=diag2(a[p + "Wv"]), awo=diag2(a[p + "Wo"].T))
    p = "L1_ffn_"
    L["grouter"] = np.concatenate([a[p + "router_w"].T] * 2, axis=0)
    gw1, gw2, gb2 = zeros(2, C, NE, C), zeros(2, C, 4, 2, C), zeros(GB, NE, GB, C)
    gw1[:] = a[p + "w1"].transpose(1, 0, 2)
    for e in range(NE):
        gw2[e % 2, :, e // 2, e % 2, :] = a[p + "w2"][e]
    for b in range(GB):
        gb2[b, :, b, :] = a[p + "b2"]
    L.update(gw1=gw1.reshape(128, -1), gw2=gw2.reshape(128, -1), gb1=a[p + "b1"].reshape(4, 128).T,
             gb2=full(gb2.reshape(64, -1)))
    packs = {}
    for name, parts in PACKS.items():
        for part, n in parts:
            assert L[part].shape == (128, n) and L[part].dtype == np.float32, (part, L[part].shape)
        packs[name] = np.ascontiguousarray(np.concatenate([L[part] for part, _ in parts], axis=1))
    return packs


def kernel(**inputs):
    import concourse.bacc as bacc
    from concourse.bass_utils import run_bass_kernel_spmd

    nc = bacc.Bacc("TRN2", target_bir_lowering=False, num_devices=1)
    arrays = {"x": np.ascontiguousarray(inputs["x"])}
    arrays.update(lay_out({k: v for k, v in inputs.items() if k != "x"}))
    args = [nc.dram_tensor(k, v.shape, F32, kind="ExternalInput").ap() for k, v in arrays.items()]
    out = nc.dram_tensor("out", (B, NT, C), F32, kind="ExternalOutput").ap()
    build(nc, *args, out, stop_after=STOP)
    return run_bass_kernel_spmd(nc, [arrays], core_ids=[0]).results[0]["out"]


STOP = 6
```

```python
from contextlib import ExitStack

import numpy as np

import concourse.bass as bass
from concourse import mybir

F32 = mybir.dt.float32
BF16 = mybir.dt.bfloat16
F32R = mybir.dt.float32r
ALU = mybir.AluOpType
ACT = mybir.ActivationFunctionType
AX = mybir.AxisListType.X

B, D_IN = 64, 8192
NT, C = 128, 64
HALF = D_IN // 2
GB = 8
NG = B // GB
PR = GB // 2
C1, C2, CQ = 16, 64, 8
L1, L2 = HALF // 8, HALF // 32
HC = 8
NH, NKV, HD = 4, 2, 16
NE = 8
HID = int(8 / 3 * C)
REM = HID - 128
RT = 3
NJ = NE + -(-NE // RT)
EPS = 1e-05
EPS_RMS = 1e-06

PACKS = {
    "tok": [("w1t", 128), ("g1row", 128), ("v1row", 128), ("w2t", 3 * 128), ("g2row", 128), ("v2row", 128),
            ("wq", 64), ("wk", 64), ("wv", 128), ("w3t", 4 * 128),
            ("cb", 3), ("cg", 3), ("cbe", 3), ("cm", 3), ("cv", 3), ("bq", 1), ("bk", 1), ("bv", 1), ("gamma", 1)],
    "const": [("ident", 128), ("headmask", 128), ("causal", 128), ("cosq", NT), ("sinq", NT), ("cosk", NT),
              ("sink", NT), ("hsel", NH), ("rev", NE), ("relumask", NT)],
    "att": [("kw", C), ("kb", C), ("vw", C), ("vb", C), ("ln1", 1), ("ln2", 1),
            ("fwq", 128), ("fwqr", 128), ("fwk", 128), ("fwkr", 128), ("fwv", 64), ("fwo", 128), ("frouter", NE),
            ("awq", 128), ("awk", 128), ("awv", 128), ("awo", 128), ("grouter", NE), ("gb1", 4), ("gb2", 2 * GB * C)],
    "moe0": [("w13", NJ * 2 * 128), ("w2", NE * C), ("w2r", (NJ - NE) * RT * C)],
    "moe1": [("gw1", 4 * 128), ("gw2", 4 * 128)],
}


def width(pack):
    return sum(n for _, n in PACKS[pack])


def wait(eng, sem, value):
    if not isinstance(value, int) or value > 0:
        eng.wait_ge(sem, value)


class PhaseSemaphores:

    def __init__(self, nc):
        self.nc, self.stack, self.held = nc, ExitStack(), []

    def __call__(self, name):
        self.held.append(self.stack.enter_context(self.nc.semaphore(name)))
        return self.held[-1]

    def __enter__(self):
        return self

    def __exit__(self, *error):
        if error[0] is None:
            with self.nc.Block() as block:
                @block.sync
                def _(sp):
                    for s in self.held:
                        sp.sem_clear(s)
        return self.stack.__exit__(*error)


class Steps:

    def __init__(self, eng, sem, n):
        self.eng, self.sem, self.n = eng, sem, n

    def begin(self, i):
        self.base, self.k = i * self.n, 0

    def __call__(self, ins):
        self.k += 1
        ins.then_inc(self.sem, 1)
        self.eng.wait_ge(self.sem, self.base + self.k)

    def end(self):
        assert self.k == self.n, self.k


def build(nc, x, tok, const, att, moe0, moe1, out, stop_after=9):
    ctx = ExitStack()
    with ctx:
        def sb(name, shape, dt=F32):
            return ctx.enter_context(nc.sbuf_tensor(name, shape, dt))

        def sem(name):
            return ctx.enter_context(nc.semaphore(name))

        PS = ctx.enter_context(nc.psum_tensor("PS", [128, 8, 512], F32))
        W = {}
        landed = {}
        packs = {}
        for name, src in (("tok", tok), ("const", const), ("att", att), ("moe0", moe0), ("moe1", moe1)):
            t = sb(f"pack_{name}", [128, width(name)])
            landed[name] = sem(f"landed_{name}") if name in ("tok", "const") else landed.get("att") or sem("landed_rest")
            packs[name] = (t, src)
            at = 0
            for part, n in PACKS[name]:
                W[part] = t[:, at:at + n]
                at += n
        H = sb("H", [128, B, C])
        FT = sb("FT", [128, B, NT])
        WT = sb("WT", [128, B, NE])
        LG = sb("LG", [128, B, NE])
        neg_half = sb("neg_half", [128, 1])
        half = sb("half", [128, 1])

        with PhaseSemaphores(nc) as phase:
            phase_tokenizer(nc, phase, x, packs, landed, W, PS, H, neg_half, half)
        if stop_after >= 2:
            with PhaseSemaphores(nc) as phase:
                phase_head_attention(nc, phase, W, PS, H, neg_half, half)
        if stop_after >= 3:
            with PhaseSemaphores(nc) as phase:
                phase_causal_attention(nc, phase, W, PS, H, FT, LG, neg_half)
        if stop_after >= 4:
            with PhaseSemaphores(nc) as phase:
                phase_swiglu_experts(nc, phase, W, PS, H, FT, WT, LG)
        if stop_after >= 5:
            with PhaseSemaphores(nc) as phase:
                phase_relu_attention(nc, phase, W, PS, H, FT, LG, neg_half)
        if stop_after >= 6:
            with PhaseSemaphores(nc) as phase:
                phase_gelu_experts(nc, phase, W, PS, H, FT, WT, LG, out)
        else:
            phase_dump(nc, H, out)


def phase_tokenizer(nc, sem, x, packs, landed, W, PS, H, neg_half, half):
    ctx = ExitStack()
    with ctx:
        def sb(name, shape, dt=F32):
            return ctx.enter_context(nc.sbuf_tensor(name, shape, dt))

        QL = HALF // 2
        xs = sb("xs", [112, QL])
        w1s = sb("w1s", [112, 128])
        w2s = sb("w2s", [128, 3, 128])
        srow = sb("srow", [128, 2, 128])
        scol = sb("scol", [128, 3])
        tcol = sb("tcol", [128, 3])
        wvg = sb("wvg", [128, 128])
        bvg = sb("bvg", [128, 1])
        h1raw = sb("h1raw", [128, L1])
        h1 = sb("h1", [128, L1 + 2])
        h2raw = sb("h2raw", [128, PR, L2])
        h2 = sb("h2", [128, PR, L2])
        qs = sb("qs", [64, PR, L2])
        ks = sb("ks", [64, PR, L2])
        vT = sb("vT", [128, PR, 128])
        nmax = sb("nmax", [128, GB])
        rowsum = sb("rowsum", [128, GB])
        rinv = sb("rinv", [128, GB])
        pexp = sb("pexp", [128, GB, 128])
        pnorm = sb("pnorm", [128, GB, 128])
        pT = sb("pT", [128, GB, 128])
        ha = sb("ha", [128, PR, L2 + 2])

        s_const = sem("s_const")
        s_rows = sem("s_rows")
        s_pow = sem("s_pow")
        s_fold = sem("s_fold")
        s_wready = sem("s_wready")
        x_in = sem("x_in")
        conv1_mm = sem("conv1_mm")
        conv1_pooled = sem("conv1_pooled")
        h1_ready = sem("h1_ready")
        conv2_mm = sem("conv2_mm")
        conv2_pooled = sem("conv2_pooled")
        h2_ready = sem("h2_ready")
        qkv_mm = sem("qkv_mm")
        qk_ready = sem("qk_ready")
        v_ready = sem("v_ready")
        energy_mm = sem("energy_mm")
        max_ready = sem("max_ready")
        exp_ready = sem("exp_ready")
        pnorm_ready = sem("pnorm_ready")
        pT_mm = sem("pT_mm")
        pT_act = sem("pT_act")
        pT_dve = sem("pT_dve")
        av_mm = sem("av_mm")
        ha_ready = sem("ha_ready")
        conv3_mm = sem("conv3_mm")
        h_written = sem("h_written")
        block = ctx.enter_context(nc.Block())
        NB = 8
        xrow = x.rearrange("b (c l) -> (b c) l", c=2)

        @block.sync
        def _(sp):
            for name in ("tok", "const", "att", "moe0", "moe1"):
                t, src = packs[name]
                sp.dma_start(t[:, :], src).then_inc(landed[name], 16)
            sp.wait_ge(s_const, 2)
            with sp.Fori(0, NG) as i:
                sp.wait_ge(conv1_mm, i * NB)
                for hf in range(2):
                    for tap in range(3):
                        lo = 1 if (hf, tap) == (0, 0) else 0
                        hi = QL - 1 if (hf, tap) == (1, 2) else QL
                        at = hf * QL + tap - 1
                        row = 64 * hf + 16 * tap
                        sp.dma_start(xs[row:row + 16, lo:hi], xrow[bass.ds(i * 16, 16), at + lo:at + hi])\
                            .then_inc(x_in, 16)
            sp.wait_ge(landed["att"], 48)

        @block.gpsimd
        def _(pool):
            nc.gpsimd.memset(neg_half[:, :], -0.5).then_inc(s_const, 1)
            pool.wait_ge(s_const, 1)
            nc.gpsimd.memset(half[:, :], 0.5).then_inc(s_rows, 1)
            pool.wait_ge(s_rows, 4)
            nc.gpsimd.tensor_tensor(srow[:, :, :], srow[:, :, :],
                                    neg_half[:, :].unsqueeze(2).broadcast_to([128, 2, 128]), ALU.pow).then_inc(s_pow, 1)
            nc.gpsimd.tensor_tensor(scol[:, :], scol[:, :],
                                    neg_half[:, :].broadcast_to([128, 3]), ALU.pow).then_inc(s_pow, 1)

        @block.tensor
        def _(pe):
            def conv1(i):
                pe.wait_ge(x_in, i * 96 + 96)
                for c in range(NB // 2):
                    for hf in range(2):
                        u = 2 * c + hf
                        if u >= 4:
                            pe.wait_ge(conv1_pooled, i * NB + u - 3)
                        lo = 64 * hf
                        nc.tensor.matmul(PS[:, u % 4, :], w1s[lo:lo + 48, :], xs[lo:lo + 48, c * 512:(c + 1) * 512],
                                         start=True, stop=True).then_inc(conv1_mm, 1)

            def conv2(i):
                pe.wait_ge(h1_ready, i + 1)
                for tap in range(3):
                    for p in range(PR):
                        mm = nc.tensor.matmul(PS[:, 4 + p, :], w2s[32 * p:32 * p + 32, tap, :],
                                              h1[32 * p:32 * p + 32, tap:tap + L1],
                                              start=(tap == 0), stop=(tap == 2))
                        if tap == 2:
                            mm.then_inc(conv2_mm, 1)

            def attention(i):
                pe.wait_ge(h2_ready, i + 1)
                nc.tensor.matmul(PS[0:64, 0, :], W["wq"], h2[:, :, :], start=True, stop=True).then_inc(qkv_mm, 1)
                nc.tensor.matmul(PS[0:64, 1, :], W["wk"], h2[:, :, :], start=True, stop=True).then_inc(qkv_mm, 1)
                for p in range(PR):
                    mm = nc.tensor.matmul(PS[:, 2, p * 128:(p + 1) * 128], h2[:, p, :], wvg[:, :],
                                          start=True, stop=True)
                mm.then_inc(qkv_mm, 1)
                pe.wait_ge(qk_ready, i * 2 + 2)
                for p in range(PR):
                    for hf in range(2):
                        r = slice(32 * hf, 32 * hf + 32)
                        mm = nc.tensor.matmul(PS[:, 4 + hf, p * 128:(p + 1) * 128], qs[r, p, :], ks[r, p, :],
                                              start=True, stop=True)
                        if p == PR - 1:
                            mm.then_inc(energy_mm, 1)
                pe.wait_ge(pnorm_ready, i * 2 + 2)
                for hf in range(2):
                    for p in range(PR):
                        mm = nc.tensor.transpose(PS[:, 6 + hf, p * 128:(p + 1) * 128],
                                                 pnorm[:, hf * PR + p, :], W["ident"])
                    mm.then_inc(pT_mm, 1)
                pe.wait_ge(v_ready, i + 1)
                pe.wait_ge(pT_act, i + 1)
                pe.wait_ge(pT_dve, i + 1)
                for p in range(PR):
                    for hf in range(2):
                        mm = nc.tensor.matmul(PS[64 * hf:64 * hf + 64, 3, p * 128:(p + 1) * 128],
                                              vT[:, p, 64 * hf:64 * hf + 64], pT[:, hf * PR + p, :],
                                              start=True, stop=True)
                mm.then_inc(av_mm, 1)
                pe.wait_ge(ha_ready, i + 1)
                for tap in range(4):
                    for hf in range(2):
                        r = slice(64 * hf, 64 * hf + 64)
                        mm = nc.tensor.matmul(PS[:, hf, 0:PR * C], W["w3t"][r, tap * 128:(tap + 1) * 128],
                                              ha[r, :, tap:tap + 2 * C - 1:2],
                                              start=(tap == 0), stop=(tap == 3))
                        if tap == 3:
                            mm.then_inc(conv3_mm, 1)

            pe.wait_ge(landed["const"], 16)
            pe.wait_ge(s_wready, 1)
            with pe.Fori(0, NG) as i:
                pe.wait_ge(h_written, i * 2)
                conv1(i)
                conv2(i)
                attention(i)

        @block.scalar
        def _(act):
            act.wait_ge(s_wready, 1)
            with act.Fori(0, NG) as i:
                act.wait_ge(conv1_pooled, i * NB + NB)
                act.wait_ge(conv2_mm, i * PR)
                nc.scalar.activation(h1[:, 1:L1 + 1], h1raw[:, :], ACT.Relu, bias=tcol[:, 0:1]).then_inc(h1_ready, 1)
                act.wait_ge(conv2_pooled, i * PR + PR)
                act.wait_ge(ha_ready, i)
                nc.scalar.activation(h2[:, :, :], h2raw[:, :, :], ACT.Relu, bias=tcol[:, 1:2]).then_inc(h2_ready, 1)
                act.wait_ge(qkv_mm, i * 3 + 1)
                nc.scalar.activation(qs[:, :, :], PS[0:64, 0, :].rearrange("p (a b) -> p a b", a=PR), ACT.Identity,
                                     bias=W["bq"][0:64]).then_inc(qk_ready, 1)
                act.wait_ge(qkv_mm, i * 3 + 2)
                nc.scalar.activation(ks[:, :, :], PS[0:64, 1, :].rearrange("p (a b) -> p a b", a=PR), ACT.Identity,
                                     bias=W["bk"][0:64]).then_inc(qk_ready, 1)
                for hf in range(2):
                    act.wait_ge(max_ready, i * 2 + hf + 1)
                    for p in range(PR):
                        u = hf * PR + p
                        nc.scalar.activation(pexp[:, u, :], PS[:, 4 + hf, p * 128:(p + 1) * 128], ACT.Exp,
                                             bias=nmax[:, u:u + 1], accum_out=rowsum[:, u:u + 1])\
                            .then_inc(exp_ready, 1)
                act.wait_ge(pT_mm, i * 2 + 1)
                nc.scalar.activation(pT[:, 0:PR, :], PS[:, 6, :].rearrange("p (a b) -> p a b", a=PR), ACT.Copy)\
                    .then_inc(pT_act, 1)
                for hf in range(2):
                    act.wait_ge(conv3_mm, i * 2 + hf + 1)
                    dst = H[:, bass.ds(i * GB, GB), :].rearrange("n (p f) t -> n p f t", f=2)[:, :, hf, :]
                    nc.scalar.activation(dst, PS[:, hf, 0:PR * C].rearrange("n (p t) -> n p t", p=PR), ACT.Identity,
                                         bias=tcol[:, 2:3], scale=scol[:, 2:3]).then_inc(h_written, 1)
            act.wait_ge(h_written, NG * 2)

        @block.vector
        def _(dve):
            dve.wait_ge(s_const, 1)
            nc.vector.memset(xs[0:16, 0:1], 0.0).then_inc(s_rows, 1)
            dve.wait_ge(s_rows, 2)
            nc.vector.memset(xs[96:112, QL - 1:QL], 0.0).then_inc(s_const, 1)
            nc.vector.memset(h1[:, 0:L1 + 2:L1 + 1], 0.0)
            nc.vector.memset(ha[:, :, 0:L2 + 2:L2 + 1], 0.0)
            dve.wait_ge(landed["tok"], 16)
            nc.vector.tensor_scalar_add(srow[:, 0, :], W["v1row"], EPS)
            nc.vector.tensor_scalar_add(srow[:, 1, :], W["v2row"], EPS).then_inc(s_rows, 1)
            nc.vector.tensor_scalar_add(scol[:, :], W["cv"], EPS).then_inc(s_rows, 1)
            dve.wait_ge(s_pow, 2)
            fold = Steps(dve, s_fold, 8)
            fold.begin(0)
            fold(nc.vector.tensor_tensor(srow[:, 0, :], srow[:, 0, :], W["g1row"], ALU.mult))
            fold(nc.vector.tensor_tensor(srow[:, 1, :], srow[:, 1, :], W["g2row"], ALU.mult))
            fold(nc.vector.tensor_tensor(scol[:, :], scol[:, :], W["cg"], ALU.mult))
            fold(nc.vector.tensor_tensor(tcol[:, :], W["cb"], W["cm"], ALU.subtract))
            fold(nc.vector.tensor_tensor(tcol[:, :], tcol[:, :], scol[:, :], ALU.mult))
            fold(nc.vector.tensor_tensor(tcol[:, :], tcol[:, :], W["cbe"], ALU.add))
            nc.vector.tensor_tensor(w1s[0:64, :], W["w1t"][0:64], srow[0:64, 0, :], ALU.mult)
            fold(nc.vector.tensor_tensor(w1s[64:112, :], W["w1t"][64:112], srow[64:112, 0, :], ALU.mult))
            nc.vector.tensor_tensor(w2s[:, :, :], W["w2t"].rearrange("p (t m) -> p t m", t=3),
                                    srow[:, 1, :].unsqueeze(1).broadcast_to([128, 3, 128]), ALU.mult)
            nc.vector.tensor_scalar(bvg[:, :], W["bv"], W["gamma"], None, ALU.mult)
            fold(nc.vector.tensor_scalar(wvg[:, :], W["wv"], W["gamma"], None, ALU.mult))
            fold.end()
            nc.vector.tensor_copy(rinv[:, 0:1], scol[:, 0:1]).then_inc(s_wready, 1)
            with dve.Fori(0, NG) as i:
                dve.wait_ge(h1_ready, i)
                for u in range(NB):
                    dve.wait_ge(conv1_mm, i * NB + u + 1)
                    at = (u % 2) * 4 + u // 2
                    nc.vector.tensor_reduce(out=h1raw[:, at * 64:(at + 1) * 64],
                                            in_=PS[:, u % 4, :].rearrange("p (a b) -> p a b", b=8),
                                            axis=AX, op=ALU.max).then_inc(conv1_pooled, 1)
                dve.wait_ge(h2_ready, i)
                for p in range(PR):
                    dve.wait_ge(conv2_mm, i * PR + p + 1)
                    nc.vector.tensor_reduce(out=h2raw[:, p, :], in_=PS[:, 4 + p, :].rearrange("p (a b) -> p a b", b=4),
                                            axis=AX, op=ALU.max).then_inc(conv2_pooled, 1)
                dve.wait_ge(qkv_mm, i * 3 + 3)
                nc.vector.tensor_copy(vT[:, :, :], PS[:, 2, :].rearrange("p (a b) -> p a b", a=PR)).then_inc(v_ready, 1)
                for hf in range(2):
                    dve.wait_ge(energy_mm, i * 2 + hf + 1)
                    nc.vector.tensor_reduce(out=nmax[:, hf * PR:(hf + 1) * PR],
                                            in_=PS[:, 4 + hf, :].rearrange("p (a b) -> p a b", a=PR),
                                            axis=AX, op=ALU.max, negate=True).then_inc(max_ready, 1)
                dve.wait_ge(exp_ready, i * GB + GB)
                nc.vector.reciprocal(rinv[:, :], rowsum[:, :]).then_inc(pnorm_ready, 1)
                dve.wait_ge(pnorm_ready, i * 2 + 1)
                nc.vector.tensor_tensor(pnorm[:, :, :], pexp[:, :, :],
                                        rinv[:, :].unsqueeze(2).broadcast_to([128, GB, 128]), ALU.mult)\
                    .then_inc(pnorm_ready, 1)
                dve.wait_ge(pT_mm, i * 2 + 2)
                nc.vector.tensor_copy(pT[:, PR:GB, :], PS[:, 7, :].rearrange("p (a b) -> p a b", a=PR))\
                    .then_inc(pT_dve, 1)
                dve.wait_ge(av_mm, i + 1)
                nc.vector.scalar_tensor_tensor(out=ha[:, :, 1:L2 + 1],
                                               in0=PS[:, 3, :].rearrange("p (a b) -> p a b", a=PR),
                                               scalar=bvg[:, 0:1], in1=h2[:, :, :],
                                               op0=ALU.add, op1=ALU.add).then_inc(ha_ready, 1)


class LayerNorm:

    def __init__(self, nc, sem, ctx, tag, neg_half):
        self.nc, self.neg_half = nc, neg_half

        def sb(name, shape):
            return ctx.enter_context(nc.sbuf_tensor(f"{tag}_{name}", shape, F32))

        self.mean = sb("mean", [128, GB])
        self.dev = sb("dev", [128, GB, C])
        self.sq = sb("sq", [128, GB, C])
        self.var = sb("var", [128, GB])
        self.rstd = sb("rstd", [128, GB])
        self.s_steps = sem(f"{tag}_steps")
        self.s_dev = sem(f"{tag}_dev_ready")
        self.s_sq = sem(f"{tag}_sq_ready")
        self.s_var = sem(f"{tag}_var_ready")
        self.s_rstd = sem(f"{tag}_rstd_ready")

    def center(self, dve, i, src):
        V = self.nc.vector
        self.step = Steps(dve, self.s_steps, 3)
        self.step.begin(i)
        self.step(V.tensor_reduce(out=self.mean[:, :], in_=src, axis=AX, op=ALU.add))
        self.step(V.tensor_scalar_mul(self.mean[:, :], self.mean[:, :], 1.0 / C))
        V.tensor_tensor(self.dev[:, :, :], src, self.mean[:, :].unsqueeze(2).broadcast_to([128, GB, C]),
                        ALU.subtract).then_inc(self.s_dev, 1)

    def variance(self, dve, i):
        V = self.nc.vector
        dve.wait_ge(self.s_sq, i + 1)
        self.step(V.tensor_reduce(out=self.var[:, :], in_=self.sq[:, :, :], axis=AX, op=ALU.add))
        self.step.end()
        V.tensor_scalar(self.var[:, :], self.var[:, :], 1.0 / C, EPS, ALU.mult, ALU.add).then_inc(self.s_var, 1)

    def normed(self, dve, i, dst):
        dve.wait_ge(self.s_rstd, i + 1)
        return self.nc.vector.tensor_tensor(dst, self.dev[:, :, :],
                                            self.rstd[:, :].unsqueeze(2).broadcast_to([128, GB, C]), ALU.mult)

    def vector(self, dve, i, src, dst):
        self.center(dve, i, src)
        self.variance(dve, i)
        return self.normed(dve, i, dst)

    def scalar(self, act, i):
        act.wait_ge(self.s_dev, i + 1)
        self.nc.scalar.activation(self.sq[:, :, :], self.dev[:, :, :], ACT.Square).then_inc(self.s_sq, 1)

    def gpsimd(self, pool, i):
        pool.wait_ge(self.s_var, i + 1)
        self.nc.gpsimd.tensor_tensor(self.rstd[:, :], self.var[:, :], self.neg_half[:, :].broadcast_to([128, GB]),
                                     ALU.pow).then_inc(self.s_rstd, 1)


class RmsNorm:

    def __init__(self, nc, sem, ctx, tag, neg_half):
        self.nc, self.neg_half = nc, neg_half

        def sb(name, shape):
            return ctx.enter_context(nc.sbuf_tensor(f"{tag}_{name}", shape, F32))

        self.sq = sb("sq", [128, GB, C])
        self.ms = sb("ms", [128, GB])
        self.rstd = sb("rstd", [128, GB])
        self.s_sq = sem(f"{tag}_sq_ready")
        self.s_ms = sem(f"{tag}_ms_ready")
        self.s_rstd = sem(f"{tag}_rstd_ready")

    def mean_square(self, dve, i):
        V = self.nc.vector
        dve.wait_ge(self.s_sq, i + 1)
        V.tensor_reduce(out=self.ms[:, :], in_=self.sq[:, :, :], axis=AX, op=ALU.add).then_inc(self.s_ms, 1)
        dve.wait_ge(self.s_ms, i * 2 + 1)
        V.tensor_scalar(self.ms[:, :], self.ms[:, :], 1.0 / C, EPS_RMS, ALU.mult, ALU.add).then_inc(self.s_ms, 1)

    def normed(self, dve, i, src, dst):
        dve.wait_ge(self.s_rstd, i + 1)
        return self.nc.vector.tensor_tensor(dst, src, self.rstd[:, :].unsqueeze(2).broadcast_to([128, GB, C]), ALU.mult)

    def scalar(self, act, i, src):
        self.nc.scalar.activation(self.sq[:, :, :], src, ACT.Square).then_inc(self.s_sq, 1)

    def gpsimd(self, pool, i):
        pool.wait_ge(self.s_ms, i * 2 + 2)
        self.nc.gpsimd.tensor_tensor(self.rstd[:, :], self.ms[:, :], self.neg_half[:, :].broadcast_to([128, GB]),
                                     ALU.pow).then_inc(self.s_rstd, 1)


class TopTwo:

    STEPS = 17

    def __init__(self, nc, sem, ctx, tag, rev, floor, op, n=B):
        self.nc, self.rev, self.floor, self.op, self.n = nc, rev, floor, op, n

        def sb(name, shape):
            return ctx.enter_context(nc.sbuf_tensor(f"{tag}_{name}", shape, F32))

        self.col = [sb(f"col{k}", [128, n]) for k in range(5)]
        self.mat = [sb(f"mat{k}", [128, n, NE]) for k in range(5)]
        self.ex = sb("ex", [128, n, NE])
        self.s_steps = sem(f"{tag}_steps")
        self.s_shift = sem(f"{tag}_shifted")
        self.s_exp = sem(f"{tag}_exp_ready")

    def vector(self, dve, i, logits, dst):
        nc, V = self.nc, self.nc.vector
        m1, den, p1, p2, kmax = (c[:, :] for c in self.col)
        lg, p, key, oh1, oh2 = (m[:, :, :] for m in self.mat)
        ex = self.ex[:, :, :]

        def wide(c):
            return c.unsqueeze(2).broadcast_to([128, self.n, NE])

        rev = self.rev.unsqueeze(1).broadcast_to([128, self.n, NE])
        step = Steps(dve, self.s_steps, self.STEPS)
        step.begin(i)
        step(V.tensor_reduce(out=m1, in_=logits, axis=AX, op=ALU.max))
        V.tensor_tensor(lg, logits, wide(m1), ALU.subtract).then_inc(self.s_shift, 1)
        dve.wait_ge(self.s_exp, i + 1)
        step(V.tensor_reduce(out=den, in_=ex, axis=AX, op=ALU.add))
        step(V.reciprocal(den, den))
        step(V.tensor_tensor(p, ex, wide(den), ALU.mult))

        def first_of_largest(src, largest, one_hot):
            step(V.tensor_reduce(out=largest, in_=src, axis=AX, op=ALU.max))
            step(V.tensor_tensor(key, src, wide(largest), ALU.is_equal))
            step(V.tensor_tensor(key, key, rev, ALU.mult))
            step(V.tensor_reduce(out=kmax, in_=key, axis=AX, op=ALU.max))
            return V.tensor_tensor(one_hot, key, wide(kmax), ALU.is_equal)

        step(first_of_largest(p, p1, oh1))
        step(V.scalar_tensor_tensor(out=lg, in0=oh1, scalar=-2.0, in1=p, op0=ALU.mult, op1=ALU.add))
        first_of_largest(lg, p2, oh2)
        V.tensor_tensor(den, p1, p2, ALU.add)
        step(V.tensor_copy(m1, p1))
        V.tensor_scalar(den, den, self.floor, None, self.op)
        step(V.tensor_tensor(oh1, oh1, oh2, ALU.add))
        V.reciprocal(den, den)
        step(V.tensor_tensor(p, p, oh1, ALU.mult))
        step.end()
        return V.tensor_tensor(dst, p, wide(den), ALU.mult)

    def scalar(self, act, i):
        act.wait_ge(self.s_shift, i + 1)
        self.nc.scalar.activation(self.ex[:, :, :], self.mat[0][:, :, :], ACT.Exp).then_inc(self.s_exp, 1)


def group(t, i):
    return t[:, bass.ds(i * GB, GB), :]


def pairs(bank):
    return bank.rearrange("p (a b) -> p a b", a=PR)


def seqs(bank):
    return bank.rearrange("p (a b) -> p a b", a=GB)


def two(t, p):
    return t[:, 2 * p:2 * p + 2, :].rearrange("p a b -> p (a b)")


def phase_head_attention(nc, sem, W, PS, H, neg_half, half):
    ctx = ExitStack()
    with ctx:
        def sb(name, shape, dt=F32):
            return ctx.enter_context(nc.sbuf_tensor(name, shape, dt))

        NHD = GB * C // HC
        ln = LayerNorm(nc, sem, ctx, "hln", neg_half)
        z = sb("b_z", [128, GB, C])
        hmean = sb("hmean", [128, NHD])
        hdev = sb("hdev", [128, NHD, HC])
        hsq = sb("hsq", [128, NHD, HC])
        hvar = sb("hvar", [128, NHD])
        hstd = sb("hstd", [128, NHD])
        hn = sb("hn", [128, GB, C])
        kt = sb("kt", [128, GB, C])
        vt = sb("vt", [128, GB, C])
        zT = sb("b_zT", [128, PR, NT])
        kvm = sb("kvm", [128, PR, 128])
        z_ready = sem("b_z_ready")
        steps = sem("b_steps")
        hdev_ready = sem("hdev_ready")
        hsq_ready = sem("hsq_ready")
        hvar_ready = sem("hvar_ready")
        hstd_ready = sem("hstd_ready")
        hn_ready = sem("hn_ready")
        k_ready = sem("b_k_ready")
        v_part = sem("b_v_part")
        v_ready = sem("b_v_ready")
        hz_added = sem("hz_added")
        zT_mm = sem("b_zT_mm")
        zT_ready = sem("b_zT_ready")
        kv_mm = sem("kv_mm")
        kvm_ready = sem("kvm_ready")
        out_mm = sem("b_out_mm")
        h_added = sem("b_h_added")
        block = ctx.enter_context(nc.Block())

        def by_head(t):
            return t[:, :, :].rearrange("p b (h d) -> p (b h) d", d=HC)

        def row(name):
            return W[name].unsqueeze(1).broadcast_to([128, GB, C])

        @block.gpsimd
        def _(pool):
            with pool.Fori(0, NG) as i:
                ln.gpsimd(pool, i)
                pool.wait_ge(z_ready, i + 1)
                nc.gpsimd.tensor_tensor(group(H, i), group(H, i), z[:, :, :], ALU.add).then_inc(hz_added, 1)
                pool.wait_ge(hvar_ready, i + 1)
                nc.gpsimd.tensor_tensor(hstd[:, :], hvar[:, :], half[:, :].broadcast_to([128, NHD]), ALU.pow)\
                    .then_inc(hstd_ready, 1)
                pool.wait_ge(hn_ready, i + 1)
                pool.wait_ge(kv_mm, i)
                nc.gpsimd.tensor_tensor(vt[:, :, :], hn[:, :, :], row("vw"), ALU.mult).then_inc(v_part, 1)
                pool.wait_ge(v_part, i + 1)
                nc.gpsimd.tensor_tensor(vt[:, :, :], vt[:, :, :], row("vb"), ALU.add).then_inc(v_ready, 1)

        @block.vector
        def _(dve):
            def front(i):
                dve.wait_ge(zT_mm, i)
                dve.wait_ge(hz_added, i)
                ln.vector(dve, i, group(H, i), z[:, :, :]).then_inc(z_ready, 1)
                dve.wait_ge(z_ready, i + 1)
                step = Steps(dve, steps, 7)
                step.begin(i)
                step(nc.vector.tensor_reduce(out=hmean[:, :], in_=by_head(z), axis=AX, op=ALU.add))
                step(nc.vector.tensor_scalar_mul(hmean[:, :], hmean[:, :], 1.0 / HC))
                nc.vector.tensor_tensor(hdev[:, :, :], by_head(z), hmean[:, :].unsqueeze(2).broadcast_to([128, NHD, HC]),
                                        ALU.subtract).then_inc(hdev_ready, 1)
                dve.wait_ge(hsq_ready, i + 1)
                step(nc.vector.tensor_reduce(out=hvar[:, :], in_=hsq[:, :, :], axis=AX, op=ALU.add))
                nc.vector.tensor_scalar_mul(hvar[:, :], hvar[:, :], 1.0 / (HC - 1)).then_inc(hvar_ready, 1)
                dve.wait_ge(hstd_ready, i + 1)
                step(nc.vector.tensor_scalar_add(hstd[:, :], hstd[:, :], EPS))
                step(nc.vector.reciprocal(hmean[:, :], hstd[:, :]))
                dve.wait_ge(v_ready, i)
                nc.vector.tensor_tensor(by_head(hn), hdev[:, :, :], hmean[:, :].unsqueeze(2).broadcast_to([128, NHD, HC]),
                                        ALU.mult).then_inc(hn_ready, 1)
                dve.wait_ge(hn_ready, i + 1)
                dve.wait_ge(kv_mm, i)
                step(nc.vector.tensor_tensor(kt[:, :, :], hn[:, :, :], row("kw"), ALU.mult))
                step(nc.vector.tensor_tensor(kt[:, :, :], kt[:, :, :], row("kb"), ALU.add))
                step.end()

            with dve.Fori(0, NG) as i:
                front(i)
                dve.wait_ge(kv_mm, i + 1)
                dve.wait_ge(out_mm, i)
                nc.vector.tensor_tensor(kvm[:, :, :], pairs(PS[:, 1, :]),
                                        W["headmask"].unsqueeze(1).broadcast_to([128, PR, 128]), ALU.mult)\
                    .then_inc(kvm_ready, 1)
                dve.wait_ge(out_mm, i + 1)
                dve.wait_ge(hz_added, i + 1)
                nc.vector.tensor_tensor(group(H, i), group(H, i), seqs(PS[:, 2, :]), ALU.add).then_inc(h_added, 1)
            dve.wait_ge(h_added, NG)

        @block.scalar
        def _(act):
            with act.Fori(0, NG) as i:
                ln.scalar(act, i)
                act.wait_ge(zT_mm, i + 1)
                act.wait_ge(out_mm, i)
                nc.scalar.activation(zT[:, :, :], pairs(PS[:, 0, :]), ACT.Copy).then_inc(zT_ready, 1)
                act.wait_ge(hdev_ready, i + 1)
                nc.scalar.activation(hsq[:, :, :], hdev[:, :, :], ACT.Square).then_inc(hsq_ready, 1)

        @block.tensor
        def _(pe):
            with pe.Fori(0, NG) as i:
                pe.wait_ge(z_ready, i + 1)
                pe.wait_ge(zT_ready, i)
                for p in range(PR):
                    mm = nc.tensor.transpose(PS[:, 0, p * 128:(p + 1) * 128], two(z, p), W["ident"])
                mm.then_inc(zT_mm, 1)
                pe.wait_ge(v_ready, i + 1)
                pe.wait_ge(steps, i * 7 + 7)
                pe.wait_ge(kvm_ready, i)
                for p in range(PR):
                    mm = nc.tensor.matmul(PS[:, 1, p * 128:(p + 1) * 128], two(kt, p), two(vt, p),
                                          start=True, stop=True)
                mm.then_inc(kv_mm, 1)
                pe.wait_ge(zT_ready, i + 1)
                pe.wait_ge(kvm_ready, i + 1)
                pe.wait_ge(h_added, i)
                for p in range(PR):
                    mm = nc.tensor.matmul(PS[:, 2, p * 128:(p + 1) * 128], zT[:, p, :], kvm[:, p, :],
                                          start=True, stop=True)
                mm.then_inc(out_mm, 1)


def split_semaphores(sem, tag):
    return {k: sem(f"{tag}_{k}")
            for k in ("f_ready", "hi_ready", "split_ready", "fT_mm", "fT_ready", "ft_stored", "router_mm")}


def phase_causal_attention(nc, sem, W, PS, H, FT, LG, neg_half):
    ctx = ExitStack()
    with ctx:
        def sb(name, shape, dt=F32):
            return ctx.enter_context(nc.sbuf_tensor(name, shape, dt))

        VW = HD + 1
        HG = GB // 2
        ln = LayerNorm(nc, sem, ctx, "cln", neg_half)
        rms1 = RmsNorm(nc, sem, ctx, "rms1", neg_half)
        rms2 = RmsNorm(nc, sem, ctx, "rms2", neg_half)
        Z = sb("c_z", [128, B, C])
        hn = sb("c_hn", [128, GB, C])
        hT = sb("c_hT", [128, PR, NT])
        rope = [sb(f"rope{n}", [128, PR, NT]) for n in range(4)]
        qT = sb("c_qT", [128, PR, NT])
        kT = sb("c_kT", [128, PR, NT])
        kblk = sb("kblk", [128, PR, 2, NH, NT])
        va = sb("va", [128, GB, NKV, VW])
        nmx = sb("nmx", [128, GB, NH])
        sh = [sb(f"sh{n}", [128, NH, NT]) for n in range(2)]
        pr = [sb(f"pr{n}", [128, NH, NT]) for n in range(3)]
        pT = [sb(f"c_pT{n}", [128, NH, NT]) for n in range(2)]
        rden = sb("rden", [128, GB * NH])
        y = sb("y", [128, GB, C])
        yT = sb("yT", [128, PR, NT])
        x2 = sb("x2", [128, GB, C])
        f = sb("c_f", [128, GB, C])
        fhl = sb("c_fhl", [128, GB, 2, C])
        fTs = sb("c_fTs", [128, GB, NT])
        wrot = sb("wrot", [128, 4, 128])
        wvn = sb("wvn", [128, 64])
        router = sb("c_router", [128, NE])
        causal_b = sb("causal_b", [128, NT], BF16)
        ident_b = sb("ident_b", [128, 128], BF16)

        w_ready = sem("c_w_ready")
        blk_zero = sem("blk_zero")
        z_ready = sem("c_z_ready")
        hn_ready = sem("c_hn_ready")
        hT_mm = sem("c_hT_mm")
        hT_ready = sem("c_hT_ready")
        proj_mm = sem("proj_mm")
        rope_ready = sem("rope_ready")
        q_ready = sem("c_q_ready")
        k_ready = sem("c_k_ready")
        kblk_in = sem("kblk_in")
        v_mm = sem("c_v_mm")
        va_ready = sem("va_ready")
        s_mm = sem("s_mm")
        max_ready = sem("c_max_ready")
        sub_ready = sem("sub_ready")
        exp_ready = sem("c_exp_ready")
        pT_mm = sem("c_pT_mm")
        pT_ready = sem("c_pT_ready")
        av_mm = sem("c_av_mm")
        rden_ready = sem("rden_ready")
        y_ready = sem("y_ready")
        yT_mm = sem("yT_mm")
        yT_ready = sem("yT_ready")
        wo_mm = sem("wo_mm")
        x2_ready = sem("x2_ready")
        h_added = sem("c_h_added")
        S = split_semaphores(sem, "c")
        lg_stored = sem("lg_stored")
        block = ctx.enter_context(nc.Block())
        wname = ["fwk", "fwkr", "fwq", "fwqr"]
        tables = ["cosk", "sink", "cosq", "sinq"]
        BANKS = (5, 0, 5, 0)

        def heads(t):
            return t.rearrange("p (h s) -> p h s", h=NH)

        @block.sync
        def _(sp):
            sp.wait_ge(blk_zero, 2)
            with sp.Fori(0, NG) as i:
                sp.wait_ge(k_ready, i + 1)
                for b in range(2):
                    for h in range(NH):
                        r = slice(64 * b + HD * h, 64 * b + HD * h + HD)
                        sp.dma_start(kblk[r, :, b, h, :], kT[r, :, :]).then_inc(kblk_in, 16)
            sp.wait_ge(kblk_in, NG * 128)

        @block.gpsimd
        def _(pool):
            def front(i):
                ln.gpsimd(pool, i)
                rms1.gpsimd(pool, i)
                wait(pool, s_mm, i * GB)
                pool.wait_ge(rope_ready, i * 4 + 2)
                nc.gpsimd.tensor_tensor(kT[:, :, :], rope[0][:, :, :], rope[1][:, :, :], ALU.add).then_inc(k_ready, 1)
                pool.wait_ge(rope_ready, i * 4 + 4)
                nc.gpsimd.tensor_tensor(qT[:, :, :], rope[2][:, :, :], rope[3][:, :, :], ALU.add).then_inc(q_ready, 1)

            def back(i):
                pool.wait_ge(x2_ready, i + 1)
                rms2.gpsimd(pool, i)
                nc.gpsimd.tensor_tensor(group(H, i), group(H, i), x2[:, :, :], ALU.add).then_inc(h_added, 1)
                split_gpsimd(nc, pool, i, S, f, fhl, fTs, FT)

            nc.gpsimd.memset(kblk[:, :, :, :, :], 0.0).then_inc(blk_zero, 1)
            nc.gpsimd.memset(va[:, :, :, HD:VW], 1.0).then_inc(blk_zero, 1)
            front(0)
            with pool.Fori(0, NG - 1) as i:
                front(i + 1)
                back(i)
            back(NG - 1)
            pool.wait_ge(h_added, NG)
            pool.wait_ge(S["ft_stored"], NG)

        @block.tensor
        def _(pe):
            def scores(i, u):
                if u % 2 == 0:
                    wait(pe, sub_ready, i * HG + u // 2)
                elif u == 1:
                    wait(pe, exp_ready, i * GB)
                else:
                    pe.wait_ge(exp_ready, i * GB + u - 1)
                if u == 0:
                    wait(pe, S["fT_ready"], i * 2)
                    pe.wait_ge(q_ready, i + 1)
                    pe.wait_ge(kblk_in, i * 128 + 128)
                nc.tensor.matmul(PS[:, 6 + u % 2, :], ident_b[:, :], causal_b[:, :].unsqueeze(1).broadcast_to([128, NH, NT]),
                                 start=True, stop=False)
                nc.tensor.matmul(PS[:, 6 + u % 2, :], qT[:, u // 2, :], kblk[:, u // 2, u % 2, :, :],
                                 start=False, stop=True).then_inc(s_mm, 1)

            def turn(i, u):
                pe.wait_ge(exp_ready, i * GB + u + 1)
                if u >= 2:
                    pe.wait_ge(pT_ready, i * GB + u - 1)
                for h in range(NH):
                    mm = nc.tensor.transpose(PS[:, 1 + u % 2, h * NT:(h + 1) * NT], pr[u % 3][:, h, :], W["ident"])
                mm.then_inc(pT_mm, 1)

            def values(i, u):
                pe.wait_ge(pT_ready, i * GB + u + 1)
                if u == 0:
                    pe.wait_ge(va_ready, i + 1)
                    wait(pe, y_ready, i * 2)
                for h in range(NH):
                    at = ((u % 4) * NH + h) * VW
                    mm = nc.tensor.matmul(PS[:, 3 + u // 4, at:at + VW], pT[u % 2][:, h, :],
                                          va[:, u, h // (NH // NKV), :], start=True, stop=True)
                mm.then_inc(av_mm, 1)

            def turn_in(i):
                wait(pe, lg_stored, i - 1)
                pe.wait_ge(hn_ready, i + 1)
                for p in range(PR):
                    mm = nc.tensor.transpose(PS[:, 0, p * 128:(p + 1) * 128], two(hn, p), W["ident"])
                mm.then_inc(hT_mm, 1)

            def project(i, n):
                if n == 0:
                    pe.wait_ge(hT_ready, i + 1)
                    wait(pe, x2_ready, i - 1)
                elif n >= 2:
                    pe.wait_ge(rope_ready, i * 4 + n - 1)
                nc.tensor.matmul(PS[:, BANKS[n], :], wrot[:, n, :], hT[:, :, :], start=True, stop=True)\
                    .then_inc(proj_mm, 1)

            def project_v(i):
                pe.wait_ge(rope_ready, i * 4 + 3)
                for p in range(PR):
                    mm = nc.tensor.matmul(PS[:, 5, p * 64:(p + 1) * 64], hT[:, p, :], wvn[:, :], start=True, stop=True)
                mm.then_inc(v_mm, 1)

            def body(i, n):
                for t in range(GB + 3):
                    if t < GB:
                        scores(i, t)
                    if 2 <= t < GB + 2:
                        turn(i, t - 2)
                    if 3 <= t:
                        values(i, t - 3)
                    if n is not None and t == 6:
                        turn_in(n)
                    if n is not None and t >= 7:
                        project(n, t - 7)
                if n is not None:
                    project_v(n)
                    pe.wait_ge(rope_ready, n * 4 + 4)
                for hf in range(2):
                    pe.wait_ge(y_ready, i * 2 + hf + 1)
                    for p in (2 * hf, 2 * hf + 1):
                        mm = nc.tensor.transpose(PS[:, 0, p * 128:(p + 1) * 128], two(y, p), W["ident"])
                mm.then_inc(yT_mm, 1)
                if n is not None:
                    pe.wait_ge(va_ready, n + 1)
                pe.wait_ge(yT_ready, i + 1)
                for p in range(PR):
                    mm = nc.tensor.matmul(PS[:, 5, p * 128:(p + 1) * 128], yT[:, p, :], W["fwo"], start=True, stop=True)
                mm.then_inc(wo_mm, 1)
                split_tensor(nc, pe, i, S, PS, (6, 7), 0, fhl, fTs, router, W["ident"])

            pe.wait_ge(w_ready, 1)
            turn_in(0)
            for n in range(4):
                project(0, n)
            project_v(0)
            with pe.Fori(0, NG - 1) as i:
                body(i, i + 1)
            body(NG - 1, None)

        @block.scalar
        def _(act):
            def expo(i, u):
                if u >= 3:
                    act.wait_ge(pT_mm, i * GB + u - 2)
                if u % 2 == 0:
                    act.wait_ge(sub_ready, i * HG + u // 2 + 1)
                    nc.scalar.activation(pr[u % 3][:, :, :], sh[u // 2 % 2][:, :, :], ACT.Exp).then_inc(exp_ready, 1)
                else:
                    act.wait_ge(max_ready, i * GB + u + 1)
                    for h in range(NH):
                        e = nc.scalar.activation(pr[u % 3][:, h, :], PS[:, 6 + u % 2, h * NT:(h + 1) * NT], ACT.Exp,
                                                 bias=nmx[:, u, h:h + 1])
                    e.then_inc(exp_ready, 1)

            def evacuate(i, u):
                act.wait_ge(pT_mm, i * GB + u + 1)
                if u >= 2:
                    act.wait_ge(av_mm, i * GB + u - 1)
                nc.scalar.activation(pT[u % 2][:, :, :], heads(PS[:, 1 + u % 2, :]), ACT.Copy).then_inc(pT_ready, 1)

            def turned_in(i):
                act.wait_ge(hT_mm, i + 1)
                nc.scalar.activation(hT[:, :, :], pairs(PS[:, 0, :]), ACT.Copy).then_inc(hT_ready, 1)

            def values_in(i):
                act.wait_ge(v_mm, i + 1)
                wait(act, av_mm, i * GB)
                nc.scalar.activation(va[:, :, :, 0:HD],
                                     PS[:, 5, 0:256].rearrange("p (b k d) -> p b k d", b=GB, k=NKV), ACT.Copy)\
                    .then_inc(va_ready, 1)

            def square_z(i):
                act.wait_ge(z_ready, i + 1)
                rms1.scalar(act, i, group(Z, i))

            def body(i, n):
                for t in range(GB + 2):
                    if t < GB:
                        expo(i, t)
                    if t >= 2:
                        evacuate(i, t - 2)
                    if n is not None and t == 1:
                        ln.scalar(act, n)
                    if n is not None and t == 4:
                        square_z(n)
                    if n is not None and t == 7:
                        turned_in(n)
                if n is not None:
                    values_in(n)
                act.wait_ge(yT_mm, i + 1)
                nc.scalar.activation(yT[:, :, :], pairs(PS[:, 0, :]), ACT.Copy).then_inc(yT_ready, 1)
                act.wait_ge(x2_ready, i + 1)
                rms2.scalar(act, i, x2[:, :, :])
                split_scalar(nc, act, i, S, PS, (6, 7), fTs)

            ln.scalar(act, 0)
            square_z(0)
            turned_in(0)
            values_in(0)
            with act.Fori(0, NG - 1) as i:
                body(i, i + 1)
            body(NG - 1, None)

        @block.vector
        def _(dve):
            def shift(i, u):
                bank = heads(PS[:, 6 + u % 2, :])
                dve.wait_ge(s_mm, i * GB + u + 1)
                nc.vector.tensor_reduce(out=nmx[:, u, :], in_=bank, axis=AX, op=ALU.max, negate=True)\
                    .then_inc(max_ready, 1)
                if u % 2 == 0:
                    dve.wait_ge(max_ready, i * GB + u + 1)
                    if u >= 4:
                        dve.wait_ge(exp_ready, i * GB + u - 3)
                    nc.vector.tensor_tensor(sh[u // 2 % 2][:, :, :], bank,
                                            nmx[:, u, :].unsqueeze(2).broadcast_to([128, NH, NT]), ALU.add)\
                        .then_inc(sub_ready, 1)

            def rotate(i, n):
                if n == 0:
                    wait(dve, k_ready, i)
                    wait(dve, q_ready, i)
                dve.wait_ge(proj_mm, i * 4 + n + 1)
                nc.vector.tensor_tensor(rope[n][:, :, :], pairs(PS[:, BANKS[n], :]),
                                        W[tables[n]].unsqueeze(1).broadcast_to([128, PR, NT]), ALU.mult)\
                    .then_inc(rope_ready, 1)

            def norm_z(i):
                ln.normed(dve, i, group(Z, i)).then_inc(z_ready, 1)

            def norm_h(i):
                wait(dve, hT_mm, i)
                rms1.normed(dve, i, group(Z, i), hn[:, :, :]).then_inc(hn_ready, 1)

            def divide(i, hf):
                dve.wait_ge(av_mm, i * GB + 4 * hf + 4)
                o = PS[:, 3 + hf, 0:4 * NH * VW].rearrange("p (a d) -> p a d", d=VW)
                rd = rden[:, hf * 4 * NH:(hf + 1) * 4 * NH]
                nc.vector.reciprocal(rd.unsqueeze(2), o[:, :, HD:VW]).then_inc(rden_ready, 1)
                dve.wait_ge(rden_ready, i * 2 + hf + 1)
                nc.vector.tensor_tensor(y[:, 4 * hf:4 * hf + 4, :].rearrange("p b (h d) -> p (b h) d", h=NH),
                                        o[:, :, 0:HD], rd.unsqueeze(2).broadcast_to([128, 4 * NH, HD]), ALU.mult)\
                    .then_inc(y_ready, 1)

            def body(i, n):
                for u in range(GB):
                    shift(i, u)
                    if n is None:
                        continue
                    if u == 0:
                        ln.center(dve, n, group(H, n))
                    if u == 2:
                        ln.variance(dve, n)
                    if u == 3:
                        norm_z(n)
                    if u == 4:
                        dve.wait_ge(z_ready, n + 1)
                        rms1.mean_square(dve, n)
                    if u == 6:
                        norm_h(n)
                divide(i, 0)
                if n is not None:
                    rotate(n, 0)
                    rotate(n, 1)
                divide(i, 1)
                if n is not None:
                    rotate(n, 2)
                    rotate(n, 3)
                dve.wait_ge(wo_mm, i + 1)
                wait(dve, h_added, i)
                nc.vector.tensor_tensor(x2[:, :, :], group(Z, i), seqs(PS[:, 5, :]), ALU.add).then_inc(x2_ready, 1)
                rms2.mean_square(dve, i)
                wait(dve, S["split_ready"], i)
                rms2.normed(dve, i, x2[:, :, :], f[:, :, :]).then_inc(S["f_ready"], 1)
                split_vector(nc, dve, i, S, f, fhl)
                dve.wait_ge(S["router_mm"], i + 1)
                nc.vector.tensor_copy(group(LG, i), PS[:, 0, 0:GB * NE].rearrange("p (b e) -> p b e", b=GB))\
                    .then_inc(lg_stored, 1)

            nc.vector.tensor_copy(causal_b[:, :], W["causal"])
            nc.vector.tensor_copy(ident_b[:, :], W["ident"])
            for n in range(4):
                nc.vector.tensor_scalar(wrot[:, n, :], W[wname[n]], W["ln1"], None, ALU.mult)
            nc.vector.tensor_scalar(wvn[:, :], W["fwv"], W["ln1"], None, ALU.mult)
            nc.vector.tensor_scalar(router[:, :], W["frouter"], W["ln2"], None, ALU.mult).then_inc(w_ready, 1)
            ln.center(dve, 0, group(H, 0))
            ln.variance(dve, 0)
            norm_z(0)
            dve.wait_ge(z_ready, 1)
            rms1.mean_square(dve, 0)
            norm_h(0)
            for n in range(4):
                rotate(0, n)
            with dve.Fori(0, NG - 1) as i:
                body(i, i + 1)
            body(NG - 1, None)
            dve.wait_ge(lg_stored, NG)


def split_vector(nc, dve, i, S, f, fhl):
    dve.wait_ge(S["f_ready"], i + 1)
    wait(dve, S["fT_mm"], i * 2)
    nc.vector.tensor_copy(fhl[:, :, 0, :].bitcast(F32R), f[:, :, :]).then_inc(S["hi_ready"], 1)


def split_gpsimd(nc, pool, i, S, f, fhl, fTs, FT):
    pool.wait_ge(S["hi_ready"], i + 1)
    nc.gpsimd.tensor_tensor(fhl[:, :, 1, :], f[:, :, :], fhl[:, :, 0, :], ALU.subtract).then_inc(S["split_ready"], 1)
    pool.wait_ge(S["fT_ready"], i * 2 + 2)
    nc.gpsimd.tensor_copy(FT[:, bass.ds(i * GB, GB), :].bitcast(F32R), fTs[:, :, :]).then_inc(S["ft_stored"], 1)


def split_tensor(nc, pe, i, S, PS, banks, logit_bank, fhl, fTs, router, ident):
    pe.wait_ge(S["split_ready"], i + 1)
    for n in range(2):
        for s in range(4):
            mm = nc.tensor.transpose(PS[:, banks[n], s * 128:(s + 1) * 128],
                                     fhl[:, 4 * n + s, :, :].rearrange("p a b -> p (a b)"), ident)
        mm.then_inc(S["fT_mm"], 1)
    pe.wait_ge(S["fT_ready"], i * 2 + 2)
    for s in range(GB):
        mm = nc.tensor.matmul(PS[:, logit_bank, s * NE:(s + 1) * NE], fTs[:, s, :], router[:, :], start=True, stop=True)
    mm.then_inc(S["router_mm"], 1)


def split_scalar(nc, act, i, S, PS, banks, fTs):
    wait(act, S["router_mm"], i)
    wait(act, S["ft_stored"], i)
    for n in range(2):
        act.wait_ge(S["fT_mm"], i * 2 + n + 1)
        nc.scalar.activation(fTs[:, 4 * n:4 * n + 4, :], pairs(PS[:, banks[n], :]), ACT.Copy).then_inc(S["fT_ready"], 1)


TS = 4
NTILE = B // TS


class Combine:

    def __init__(self, nc, sem, ctx, tag, PS, WT, down_mm):
        self.nc, self.PS, self.WT, self.down_mm = nc, PS, WT, down_mm
        self.ws = ctx.enter_context(nc.sbuf_tensor(f"{tag}_ws", [128, TS, NE], F32))
        self.tmp = [ctx.enter_context(nc.sbuf_tensor(f"{tag}_tmp{n}", [128, NE, C], F32)) for n in range(2)]
        self.ys = ctx.enter_context(nc.sbuf_tensor(f"{tag}_ys", [128, TS, C], F32))
        self.ws_ready = sem(f"{tag}_ws_ready")
        self.mult = sem(f"{tag}_comb_mult")
        self.red = sem(f"{tag}_comb_red")

    def weights(self, pool, i):
        wait(pool, self.red, i * TS)
        self.nc.gpsimd.tensor_copy(self.ws[:, :, :], self.WT[:, bass.ds(i * TS, TS), :]).then_inc(self.ws_ready, 1)

    def vector(self, dve, i, q, taken):
        V = self.nc.vector
        if q == 0:
            dve.wait_ge(self.ws_ready, i + 1)
        dve.wait_ge(self.down_mm, i * TS + q + 1)
        V.tensor_tensor(self.tmp[q % 2][:, :, :], self.PS[:, 6 + q % 2, :].rearrange("p (e c) -> p e c", e=NE),
                        self.ws[:, q, :].unsqueeze(2).broadcast_to([128, NE, C]), ALU.mult).then_inc(self.mult, 1)
        dve.wait_ge(self.mult, i * TS + q + 1)
        if q == 0:
            wait(dve, taken, i)
        V.tensor_reduce(out=self.ys[:, q, :], in_=self.tmp[q % 2][:, :, :].rearrange("p e c -> p c e"),
                        axis=AX, op=ALU.add).then_inc(self.red, 1)

    def bank_free(self, pe, i, q):
        if q >= 2:
            pe.wait_ge(self.mult, i * TS + q - 1)
        else:
            wait(pe, self.mult, i * TS)


def tiles(eng, step):
    step((0, 0), None)
    with eng.Fori(0, NTILE // 2 - 1) as k:
        step((k * 2 + 1, 1), (k * 2, 0))
        step((k * 2 + 2, 0), (k * 2 + 1, 1))
    step((NTILE - 1, 1), (NTILE - 2, 0))
    step(None, (NTILE - 1, 1))


def phase_swiglu_experts(nc, sem, W, PS, H, FT, WT, LG):
    ctx = ExitStack()
    with ctx:
        def sb(name, shape, dt=F32):
            return ctx.enter_context(nc.sbuf_tensor(name, shape, dt))

        wh = sb("d_wh", [128, NJ, 2, 128])
        wl = sb("d_wl", [128, NJ, 2, 128])
        sa = [sb(f"sa{n}", [128, 512]) for n in range(3)]
        hh = [sb(f"hh{n}", [128, NJ, 512]) for n in range(2)]
        w_steps = sem("d_w_steps")
        up_mm = sem("up_mm")
        silu_ready = sem("silu_ready")
        hh_ready = sem("hh_ready")
        down_mm = sem("down_mm")
        h_added = sem("d_h_added")
        wt_ready = sem("d_wt_ready")
        comb = Combine(nc, sem, ctx, "d", PS, WT, down_mm)
        top = TopTwo(nc, sem, ctx, "dtop", W["rev"], 1e-9, ALU.add)
        block = ctx.enter_context(nc.Block())
        w13 = W["w13"].rearrange("p (j n m) -> p j n m", j=NJ, n=2)
        w2 = W["w2"].rearrange("p (e c) -> p e c", e=NE)
        w2r = W["w2r"].rearrange("p (t c) -> p t c", t=NJ - NE)
        ft = FT[:, :, :].rearrange("p b t -> p (b t)")
        AFTER = {2: 0, 5: 1, 8: 2, 10: 3}

        @block.gpsimd
        def _(pool):
            pool.wait_ge(wt_ready, 1)
            with pool.Fori(0, NTILE) as i:
                comb.weights(pool, i)
                pool.wait_ge(comb.red, i * TS + TS)
                h = H[:, bass.ds(i * TS, TS), :]
                nc.gpsimd.tensor_tensor(h, h, comb.ys[:, :, :], ALU.add).then_inc(h_added, 1)
            pool.wait_ge(h_added, NTILE)

        @block.tensor
        def _(pe):
            def up(i, j):
                s = j % 3
                if j >= 3:
                    pe.wait_ge(hh_ready, i * NJ + j - 2)
                else:
                    wait(pe, hh_ready, i * NJ)
                for n in range(2):
                    for k, w in enumerate((wh, wl)):
                        mm = nc.tensor.matmul(PS[:, 2 * s + n, :], w[:, j, n, :].bitcast(F32R),
                                              ft[:, bass.ds(i * 512, 512)].bitcast(F32R), start=(k == 0), stop=(k == 1))
                    mm.then_inc(up_mm, 1)

            def down(i, buf, q):
                if q == 0:
                    pe.wait_ge(hh_ready, i * NJ + NJ)
                comb.bank_free(pe, i, q)
                o = PS[:, 6 + q % 2, :]
                for t in range(NJ - NE):
                    es = range(t * RT, min((t + 1) * RT, NE))
                    nc.tensor.matmul(o[:, es[0] * C:(es[-1] + 1) * C], hh[buf][:, NE + t, q * NT:(q + 1) * NT],
                                     w2r[:, t, 0:len(es) * C], start=True, stop=False)
                    for e in es:
                        mm = nc.tensor.matmul(o[:, e * C:(e + 1) * C], hh[buf][:, e, q * NT:(q + 1) * NT], w2[:, e, :],
                                              start=False, stop=(e == es[-1]))
                mm.then_inc(down_mm, 1)

            def step(a, b):
                for j in range(NJ):
                    if a:
                        up(a[0], j)
                    if b and j in AFTER:
                        down(b[0], b[1], AFTER[j])

            pe.wait_ge(w_steps, 3)
            tiles(pe, step)

        @block.scalar
        def _(act):
            def step(a, b):
                if not a:
                    return
                i = a[0]
                for j in range(NJ):
                    act.wait_ge(up_mm, i * 2 * NJ + 2 * j + 1)
                    if j >= 3:
                        act.wait_ge(hh_ready, i * NJ + j - 2)
                    else:
                        wait(act, hh_ready, i * NJ)
                    nc.scalar.activation(sa[j % 3][:, :], PS[:, 2 * (j % 3), :], ACT.Silu).then_inc(silu_ready, 1)

            top.scalar(act, 0)
            tiles(act, step)

        @block.vector
        def _(dve):
            def step(a, b):
                for j in range(NJ):
                    if a:
                        i, buf = a
                        if j == 0 and b:
                            wait(dve, down_mm, (i - 1) * TS)
                        dve.wait_ge(silu_ready, i * NJ + j + 1)
                        dve.wait_ge(up_mm, i * 2 * NJ + 2 * j + 2)
                        nc.vector.tensor_tensor(hh[buf][:, j, :], PS[:, 2 * (j % 3) + 1, :], sa[j % 3][:, :], ALU.mult)\
                            .then_inc(hh_ready, 1)
                    if b and j in AFTER:
                        comb.vector(dve, b[0], AFTER[j], h_added)

            nc.vector.tensor_scalar(w13, w13, W["ln2"], None, ALU.mult).then_inc(w_steps, 1)
            dve.wait_ge(w_steps, 1)
            nc.vector.tensor_copy(wh[:, :, :, :].bitcast(F32R), w13).then_inc(w_steps, 1)
            dve.wait_ge(w_steps, 2)
            nc.vector.tensor_tensor(wl[:, :, :, :].bitcast(F32R), w13, wh[:, :, :, :], ALU.subtract).then_inc(w_steps, 1)
            top.vector(dve, 0, LG[:, :, :], WT[:, :, :]).then_inc(wt_ready, 1)
            tiles(dve, step)


def phase_relu_attention(nc, sem, W, PS, H, FT, LG, neg_half):
    ctx = ExitStack()
    with ctx:
        def sb(name, shape, dt=F32):
            return ctx.enter_context(nc.sbuf_tensor(name, shape, dt))

        ln3 = LayerNorm(nc, sem, ctx, "ln3", neg_half)
        ln4 = LayerNorm(nc, sem, ctx, "ln4", neg_half)
        wqk = sb("wqk", [128, 2, 128])
        wvo = sb("wvo", [128, 128])
        z = sb("e_z", [128, GB, C])
        zT = sb("e_zT", [128, PR, NT])
        uT = sb("uT", [128, PR, 2, NT])
        vs = sb("e_vs", [128, GB, C])
        pm = sb("pm", [128, GB, NT])
        h2 = sb("e_h2", [128, GB, C])
        z4 = sb("z4", [128, GB, C])
        fhl = sb("e_fhl", [128, GB, 2, C])
        fTs = sb("e_fTs", [128, GB, NT])
        w_mm = sem("e_w_mm")
        w_ready = sem("e_w_ready")
        z_ready = sem("e_z_ready")
        zT_mm = sem("e_zT_mm")
        zT_ready = sem("e_zT_ready")
        u_mm = sem("e_u_mm")
        u_ready = sem("e_u_ready")
        v_mm = sem("e_v_mm")
        v_ready = sem("e_v_ready")
        s_mm = sem("e_s_mm")
        pm_ready = sem("pm_ready")
        av_mm = sem("e_av_mm")
        h2_ready = sem("e_h2_ready")
        S = split_semaphores(sem, "e")
        lg_stored = sem("e_lg_stored")
        h_stored = sem("e_h_stored")
        block = ctx.enter_context(nc.Block())

        @block.gpsimd
        def _(pool):
            def back(i):
                ln4.gpsimd(pool, i)
                pool.wait_ge(S["f_ready"], i + 1)
                nc.gpsimd.tensor_tensor(group(H, i), z4[:, :, :], h2[:, :, :], ALU.add).then_inc(h_stored, 1)
                split_gpsimd(nc, pool, i, S, z4, fhl, fTs, FT)

            ln3.gpsimd(pool, 0)
            with pool.Fori(0, NG - 1) as i:
                ln3.gpsimd(pool, i + 1)
                back(i)
            back(NG - 1)
            pool.wait_ge(h_stored, NG)
            pool.wait_ge(S["ft_stored"], NG)

        @block.tensor
        def _(pe):
            def turn_in(i):
                pe.wait_ge(z_ready, i + 1)
                wait(pe, h2_ready, i - 1)
                for p in range(PR):
                    mm = nc.tensor.transpose(PS[:, 0, p * 128:(p + 1) * 128], two(z, p), W["ident"])
                mm.then_inc(zT_mm, 1)

            def project(i):
                pe.wait_ge(zT_ready, i + 1)
                wait(pe, lg_stored, i - 1)
                for b in range(2):
                    nc.tensor.matmul(PS[:, 1 + b, :], wqk[:, b, :], zT[:, :, :], start=True, stop=True)\
                        .then_inc(u_mm, 1)

            def project_v(i):
                wait(pe, v_ready, i)
                for p in range(PR):
                    mm = nc.tensor.matmul(PS[:, 3, p * 128:(p + 1) * 128], zT[:, p, :], wvo[:, :], start=True, stop=True)
                mm.then_inc(v_mm, 1)

            def body(i, n):
                pe.wait_ge(u_ready, i * 2 + 2)
                for p in range(PR):
                    if p == 0:
                        wait(pe, pm_ready, i * 2)
                    mm = nc.tensor.matmul(PS[:, 4 + p // 2, (p % 2) * 256:(p % 2) * 256 + 256], zT[:, p, :], uT[:, p, :, :],
                                          start=True, stop=True)
                    if p % 2:
                        mm.then_inc(s_mm, 1)
                if n is not None:
                    turn_in(n)
                    project(n)
                    project_v(n)
                pe.wait_ge(v_ready, i + 1)
                for s in range(GB):
                    if s % 4 == 0:
                        pe.wait_ge(pm_ready, i * 2 + s // 4 + 1)
                    mm = nc.tensor.matmul(PS[:, 0, s * C:(s + 1) * C], pm[:, s, :], vs[:, s, :], start=True, stop=True)
                mm.then_inc(av_mm, 1)
                if n is not None:
                    pe.wait_ge(u_ready, n * 2 + 1)
                split_tensor(nc, pe, i, S, PS, (6, 7), 1, fhl, fTs, W["grouter"], W["ident"])

            nc.tensor.matmul(PS[:, 0, 0:128], W["awq"], W["awk"], start=True, stop=True).then_inc(w_mm, 1)
            nc.tensor.matmul(PS[:, 1, 0:128], W["awv"], W["awo"], start=True, stop=True).then_inc(w_mm, 1)
            pe.wait_ge(w_ready, 3)
            turn_in(0)
            project(0)
            project_v(0)
            with pe.Fori(0, NG - 1) as i:
                body(i, i + 1)
            body(NG - 1, None)

        @block.scalar
        def _(act):
            def turned_in(i):
                act.wait_ge(zT_mm, i + 1)
                wait(act, s_mm, i * 2)
                nc.scalar.activation(zT[:, :, :], pairs(PS[:, 0, :]), ACT.Copy).then_inc(zT_ready, 1)

            def projected(i):
                for b in range(2):
                    act.wait_ge(u_mm, i * 2 + b + 1)
                    nc.scalar.activation(uT[:, :, b, :], pairs(PS[:, 1 + b, :]), ACT.Copy).then_inc(u_ready, 1)

            def values_in(i):
                act.wait_ge(v_mm, i + 1)
                wait(act, av_mm, i)
                nc.scalar.activation(vs[:, :, :], seqs(PS[:, 3, :]), ACT.Copy).then_inc(v_ready, 1)

            def body(i, n):
                if n is not None:
                    ln3.scalar(act, n)
                    turned_in(n)
                    projected(n)
                ln4.scalar(act, i)
                if n is not None:
                    values_in(n)
                split_scalar(nc, act, i, S, PS, (6, 7), fTs)

            ln3.scalar(act, 0)
            turned_in(0)
            projected(0)
            values_in(0)
            with act.Fori(0, NG - 1) as i:
                body(i, i + 1)
            body(NG - 1, None)

        @block.vector
        def _(dve):
            def norm3(i):
                ln3.variance(dve, i)
                wait(dve, zT_mm, i)
                ln3.normed(dve, i, z[:, :, :]).then_inc(z_ready, 1)

            def mask(i, n):
                dve.wait_ge(s_mm, i * 2 + n + 1)
                nc.vector.scalar_tensor_tensor(out=pm[:, 4 * n:4 * n + 4, :], in0=pairs(PS[:, 4 + n, :]), scalar=0.0,
                                               in1=W["relumask"].unsqueeze(1).broadcast_to([128, 4, NT]),
                                               op0=ALU.max, op1=ALU.mult).then_inc(pm_ready, 1)

            def body(i, n):
                if n is not None:
                    ln3.center(dve, n, group(H, n))
                mask(i, 0)
                if n is not None:
                    norm3(n)
                mask(i, 1)
                dve.wait_ge(av_mm, i + 1)
                wait(dve, h_stored, i)
                nc.vector.tensor_tensor(h2[:, :, :], group(H, i), seqs(PS[:, 0, :]), ALU.add).then_inc(h2_ready, 1)
                dve.wait_ge(h2_ready, i + 1)
                ln4.center(dve, i, h2[:, :, :])
                ln4.variance(dve, i)
                wait(dve, S["split_ready"], i)
                ln4.normed(dve, i, z4[:, :, :]).then_inc(S["f_ready"], 1)
                split_vector(nc, dve, i, S, z4, fhl)
                dve.wait_ge(S["router_mm"], i + 1)
                nc.vector.tensor_copy(group(LG, i), PS[:, 1, 0:GB * NE].rearrange("p (b e) -> p b e", b=GB))\
                    .then_inc(lg_stored, 1)

            dve.wait_ge(w_mm, 2)
            nc.vector.memset(wqk[:, :, :], 0.0).then_inc(w_ready, 1)
            dve.wait_ge(w_ready, 1)
            nc.vector.tensor_copy(wqk[0:64, 0, 0:64], PS[0:64, 0, 0:64])
            nc.vector.tensor_copy(wqk[64:128, 1, 64:128], PS[64:128, 0, 64:128]).then_inc(w_ready, 1)
            nc.vector.tensor_copy(wvo[:, :], PS[:, 1, 0:128]).then_inc(w_ready, 1)
            ln3.center(dve, 0, group(H, 0))
            norm3(0)
            with dve.Fori(0, NG - 1) as i:
                body(i, i + 1)
            body(NG - 1, None)
            dve.wait_ge(lg_stored, NG)


def phase_gelu_experts(nc, sem, W, PS, H, FT, WT, LG, out):
    ctx = ExitStack()
    with ctx:
        def sb(name, shape, dt=F32):
            return ctx.enter_context(nc.sbuf_tensor(name, shape, dt))

        NK = NE // 2
        NW = B * NE // 128
        wh = sb("f_wh", [128, NK, 128])
        wl = sb("f_wl", [128, NK, 128])
        gg = [sb(f"gg{n}", [128, NK, 512]) for n in range(2)]
        fin = [sb(f"fin{n}", [128, TS, C]) for n in range(2)]
        wTs = sb("wTs", [128, NW, NT])
        w_steps = sem("f_w_steps")
        up_mm = sem("f_up_mm")
        gg_ready = sem("gg_ready")
        down_mm = sem("f_down_mm")
        wt_ready = sem("f_wt_ready")
        wT_mm = sem("wT_mm")
        wT_ready = sem("wT_ready")
        b2_mm = sem("b2_mm")
        b2_added = sem("b2_added")
        fin_ready = sem("fin_ready")
        stored = sem("out_stored")
        comb = Combine(nc, sem, ctx, "f", PS, WT, down_mm)
        top = TopTwo(nc, sem, ctx, "ftop", W["rev"], 1e-12, ALU.max)
        block = ctx.enter_context(nc.Block())
        w1 = W["gw1"].rearrange("p (j m) -> p j m", j=NK)
        w2 = W["gw2"].rearrange("p (j m) -> p j m", j=NK)
        b2 = W["gb2"].rearrange("p (n m) -> p n m", n=2)
        ft = FT[:, :, :].rearrange("p b t -> p (b t)")
        ov = out.rearrange("b n t -> n b t")

        @block.sync
        def _(sp):
            with sp.Fori(0, NTILE // 2) as k:
                for n in range(2):
                    sp.wait_ge(fin_ready, k * 2 + n + 1)
                    sp.dma_start(ov[:, bass.ds((k * 2 + n) * TS, TS), :], fin[n][:, :, :]).then_inc(stored, 16)
            sp.wait_ge(stored, NTILE * 16)

        @block.gpsimd
        def _(pool):
            pool.wait_ge(wt_ready, 1)
            pool.wait_ge(b2_added, 2 * NW)
            with pool.Fori(0, NTILE // 2) as k:
                for n in range(2):
                    i = k * 2 + n
                    comb.weights(pool, i)
                    pool.wait_ge(comb.red, i * TS + TS)
                    if n == 0:
                        pool.wait_ge(stored, k * 32)
                    else:
                        pool.wait_ge(stored, k * 32)
                    nc.gpsimd.tensor_tensor(fin[n][:, :, :], H[:, bass.ds(i * TS, TS), :], comb.ys[:, :, :], ALU.add)\
                        .then_inc(fin_ready, 1)

        @block.tensor
        def _(pe):
            def up(i, j):
                wait(pe, gg_ready, (i - 1) * NK + j + 1)
                for k, w in enumerate((wh, wl)):
                    mm = nc.tensor.matmul(PS[:, j, :], w[:, j, :].bitcast(F32R),
                                          ft[:, bass.ds(i * 512, 512)].bitcast(F32R), start=(k == 0), stop=(k == 1))
                mm.then_inc(up_mm, 1)

            def down(i, buf, q):
                if q == 0:
                    pe.wait_ge(gg_ready, i * NK + NK)
                comb.bank_free(pe, i, q)
                for j in range(NK):
                    mm = nc.tensor.matmul(PS[:, 6 + q % 2, j * 128:(j + 1) * 128], gg[buf][:, j, q * NT:(q + 1) * NT],
                                          w2[:, j, :], start=True, stop=True)
                mm.then_inc(down_mm, 1)

            def step(a, b):
                for j in range(NK):
                    if a:
                        up(a[0], j)
                    if b:
                        down(b[0], b[1], j)

            pe.wait_ge(w_steps, 2)
            pe.wait_ge(wt_ready, 1)
            wt = WT[:, :, :].rearrange("p b e -> p (b e)")
            for n in range(NW):
                mm = nc.tensor.transpose(PS[:, 4, n * 128:(n + 1) * 128], wt[:, n * 128:(n + 1) * 128], W["ident"])
            mm.then_inc(wT_mm, 1)
            pe.wait_ge(wT_ready, 1)
            for n in range(2 * NW):
                if n >= 2:
                    pe.wait_ge(b2_added, n - 1)
                nc.tensor.matmul(PS[:, 4 + n % 2, :], wTs[:, n // 2, :], b2[:, n % 2, :], start=True, stop=True)\
                    .then_inc(b2_mm, 1)
            tiles(pe, step)

        @block.scalar
        def _(act):
            def step(a, b):
                if not a:
                    return
                i, buf = a
                for j in range(NK):
                    act.wait_ge(up_mm, i * NK + j + 1)
                    if j == 0 and b:
                        wait(act, down_mm, (i - 1) * TS)
                    nc.scalar.activation(gg[buf][:, j, :], PS[:, j, :], ACT.Gelu, bias=W["gb1"][:, j:j + 1])\
                        .then_inc(gg_ready, 1)

            top.scalar(act, 0)
            act.wait_ge(wT_mm, 1)
            nc.scalar.activation(wTs[:, :, :], PS[:, 4, :].rearrange("p (a b) -> p a b", a=NW), ACT.Copy)\
                .then_inc(wT_ready, 1)
            tiles(act, step)

        @block.vector
        def _(dve):
            def step(a, b):
                if b:
                    for q in range(TS):
                        comb.vector(dve, b[0], q, fin_ready)

            nc.vector.tensor_copy(wh[:, :, :].bitcast(F32R), w1).then_inc(w_steps, 1)
            dve.wait_ge(w_steps, 1)
            nc.vector.tensor_tensor(wl[:, :, :].bitcast(F32R), w1, wh[:, :, :], ALU.subtract).then_inc(w_steps, 1)
            top.vector(dve, 0, LG[:, :, :], WT[:, :, :]).then_inc(wt_ready, 1)
            for n in range(2 * NW):
                dve.wait_ge(b2_mm, n + 1)
                nc.vector.tensor_tensor(H[:, n * GB:(n + 1) * GB, :], H[:, n * GB:(n + 1) * GB, :],
                                        seqs(PS[:, 4 + n % 2, :]), ALU.add).then_inc(b2_added, 1)
            tiles(dve, step)


def phase_dump(nc, H, out):
    ctx = ExitStack()
    with ctx:
        done = ctx.enter_context(nc.semaphore("dumped"))
        block = ctx.enter_context(nc.Block())

        @block.sync
        def _(sp):
            sp.dma_start(out.rearrange("b n t -> n b t"), H[:, :, :]).then_inc(done, 16)
            sp.wait_ge(done, 16)


def constants():
    r = np.arange(128)
    inv_freq = 1.0 / 10000.0 ** (np.arange(0, HD, 2, dtype=np.float32) / HD)
    freqs = np.outer(np.arange(NT, dtype=np.float32), inv_freq)
    emb = np.concatenate([freqs, freqs], axis=-1)
    d = r % HD
    cos, sin = np.cos(emb).T[d].astype(np.float32), np.sin(emb).T[d].astype(np.float32)
    sin = np.where((d < HD // 2)[:, None], -sin, sin)
    head = (r % 64) // HD
    c = {
        "ident": np.eye(128),
        "headmask": (r[:, None] // HC == r[None, :] // HC) / NT,
        "causal": np.where(r[None, :] <= r[:, None], 0.0, -1e30),
        "cosq": cos / np.sqrt(HD), "sinq": sin / np.sqrt(HD), "cosk": cos, "sink": sin,
        "hsel": head[:, None] == np.arange(NH)[None, :],
        "rev": np.broadcast_to(np.arange(NE, 0, -1), (128, NE)),
        "relumask": (r[:, None] <= r[None, :]) / np.maximum(r[None, :], 1),
    }
    return {k: np.asarray(v, np.float32) for k, v in c.items()}


def lay_out(a):
    a = {k: np.asarray(v) for k, v in a.items()}

    def zeros(*s):
        return np.zeros(s, np.float32)

    def diag2(m):
        k, n = m.shape
        o = zeros(2 * k, 2 * n)
        o[:k, :n] = m
        o[k:, n:] = m
        return o

    def col(v, n):
        return np.tile(v, n)[:, None]

    p = "L0_tok_"
    L = constants()
    w1, w2 = a[p + "w1"], a[p + "w2"]
    w1t = zeros(2, 64, GB, C1)
    w2t = zeros(PR, 2, C1, 3, 2, C2)
    for b in range(GB):
        for tap in range(3):
            at = tap * 16 + b * 2
            w1t[:, at:at + 2, b, :] = w1[:, :, tap].T
    for b in range(2):
        w2t[:, b, :, :, b, :] = w2.transpose(1, 2, 0)
    L["w1t"] = w1t.reshape(128, 128)
    L["w2t"] = w2t.reshape(128, 3 * 128)
    for n, reps in (("1", GB), ("2", 2)):
        for k in "gv":
            L[f"{k}{n}row"] = np.broadcast_to(np.tile(a[p + k + n], reps)[None, :], (128, 128))
    wq, wk = zeros(128, 64), zeros(128, 64)
    bq, bk = zeros(128, 1), zeros(128, 1)
    for b in range(2):
        wq[64 * b:64 * b + 64, 32 * b:32 * b + CQ] = a[p + "wq"].T
        wk[64 * b:64 * b + 64, 32 * b:32 * b + CQ] = a[p + "wk"].T
        bq[32 * b:32 * b + CQ, 0] = a[p + "bq"]
        bk[32 * b:32 * b + CQ, 0] = a[p + "bk"]
    L.update(wq=wq, wk=wk, bq=bq, bk=bk, wv=diag2(a[p + "wv"].T), bv=col(a[p + "bv"], 2))
    w3 = a[p + "w3"].transpose(1, 2, 0).reshape(C2, 4 * 128)
    L["w3t"] = np.concatenate([w3, w3], axis=0)
    L["gamma"] = np.broadcast_to(a[p + "gamma"].reshape(1, 1), (128, 1))
    for k in ("b", "g", "be", "m", "v"):
        L["c" + k] = np.concatenate([col(a[f"{p}{k}1"], GB), col(a[f"{p}{k}2"], 2), col(a[f"{p}{k}3"], 1)], axis=1)
    p = "L0_attn_"
    for k, n in (("kw", "kln_weight"), ("kb", "kln_bias"), ("vw", "vln_weight"), ("vb", "vln_bias")):
        L[k] = np.broadcast_to(a[p + n].reshape(1, C), (128, C))
    p = "L0_ffn_"
    L["ln1"], L["ln2"] = col(a[p + "ln1_w"], 2), col(a[p + "ln2_w"], 2)
    q = a[p + "wq"].reshape(NH, HD, C)
    k = np.repeat(a[p + "wk"].reshape(NKV, HD, C), NH // NKV, axis=0)
    for n, m in (("q", q), ("k", k)):
        L["fw" + n] = diag2(m.reshape(NH * HD, C).T)
        L["fw" + n + "r"] = diag2(np.concatenate([m[:, HD // 2:], m[:, :HD // 2]], axis=1).reshape(NH * HD, C).T)
    L["fwv"] = diag2(a[p + "wv"].T)
    L["fwo"] = diag2(a[p + "wo"].T)
    L["frouter"] = np.concatenate([a[p + "router_w"].T] * 2, axis=0)
    w13, w2m, w2r = zeros(2, C, NJ, 2, 128), zeros(128, NE, C), zeros(128, NJ - NE, RT, C)
    for e in range(NE):
        t, s = NE + e // RT, e % RT
        for n, w in enumerate((a[p + "w1"][e], a[p + "w3"][e])):
            w13[:, :, e, n, :] = w[:128].T
            w13[:, :, t, n, s * REM:(s + 1) * REM] = w[128:].T
        w = a[p + "w2"][e].T
        w2m[:, e] = w[:128]
        w2r[s * REM:(s + 1) * REM, e // RT, s] = w[128:]
    L.update(w13=w13.reshape(128, -1), w2=w2m.reshape(128, -1), w2r=w2r.reshape(128, -1))
    p = "L1_attn_"
    L.update(awq=diag2(a[p + "Wq"]), awk=diag2(a[p + "Wk"]), awv=diag2(a[p + "Wv"]), awo=diag2(a[p + "Wo"].T))
    p = "L1_ffn_"
    L["grouter"] = np.concatenate([a[p + "router_w"].T] * 2, axis=0)
    gw1, gw2, gb2 = zeros(2, C, NE, C), zeros(2, C, 4, 2, C), zeros(2, GB, NE, 2, GB, C)
    gw1[:] = a[p + "w1"].transpose(1, 0, 2)
    for e in range(NE):
        gw2[e % 2, :, e // 2, e % 2, :] = a[p + "w2"][e]
    for b in range(GB):
        for n in range(2):
            gb2[n, b, :, n, b, :] = a[p + "b2"]
    L.update(gw1=gw1.reshape(128, -1), gw2=gw2.reshape(128, -1), gb1=a[p + "b1"].reshape(4, 128).T,
             gb2=gb2.reshape(128, -1))
    packs = {}
    for name, parts in PACKS.items():
        for part, n in parts:
            assert L[part].shape == (128, n) and L[part].dtype == np.float32, (part, L[part].shape)
        packs[name] = np.ascontiguousarray(np.concatenate([L[part] for part, _ in parts], axis=1))
    return packs


def kernel(**inputs):
    import concourse.bacc as bacc
    from concourse.bass_utils import run_bass_kernel_spmd

    nc = bacc.Bacc("TRN2", target_bir_lowering=False, num_devices=1)
    arrays = {"x": np.ascontiguousarray(inputs["x"])}
    arrays.update(lay_out({k: v for k, v in inputs.items() if k != "x"}))
    args = [nc.dram_tensor(k, v.shape, F32, kind="ExternalInput").ap() for k, v in arrays.items()]
    out = nc.dram_tensor("out", (B, NT, C), F32, kind="ExternalOutput").ap()
    build(nc, *args, out, stop_after=STOP)
    return run_bass_kernel_spmd(nc, [arrays], core_ids=[0]).results[0]["out"]


STOP = 6
```
